# Optimizing a Trainium2 kernel written in Bass

```python
import numpy as np
import jax
import jax.numpy as jnp

def _softmax(x, axis=-1):
    return jax.nn.softmax(x, axis=axis)

def _gelu(x):
    return jax.nn.gelu(x, approximate=True)

def _silu(x):
    return jax.nn.silu(x)

def _sigmoid(x):
    return jax.nn.sigmoid(x)

def _layernorm(x, axis=-1, eps=1e-05):
    m = jnp.mean(x, axis=axis, keepdims=True)
    v = jnp.var(x, axis=axis, keepdims=True)
    return (x - m) / jnp.sqrt(v + eps)

def _scatter_add(tgt, idx, src, axis=0):
    return tgt.at[idx].add(src)

def _segment_sum(src, seg, n):
    return jax.ops.segment_sum(src, seg, n)
kernel_name = 'mk_decoder_preln_d1_seqx_r8_ea71b9'

def setup_inputs(seed: int=0):
    np.random.seed(seed)
    _w = jnp.asarray

    def _rec_inputs():
        import jax
        import jax.numpy as jnp
        _rk = jax.random.key(seed)
        x = -0.0002928 + 1 * jax.random.normal(jax.random.fold_in(_rk, 1), (16, 128, 256), jnp.float32)
        _lenS = 128 - jax.random.randint(jax.random.fold_in(_rk, 7), (16,), 0, max(1, 128 // 4) + 1, jnp.int32)
        _lenS2 = 128 - jax.random.randint(jax.random.fold_in(_rk, 8), (16,), 0, max(1, 128 // 4) + 1, jnp.int32)
        fside_S2_0 = -0.00337071 + 1.01897 * jax.random.normal(jax.random.fold_in(_rk, 11), (128,), jnp.float32)
        _ctx_2048P = jax.random.normal(jax.random.fold_in(_rk, 12), (16, 16, 256), jnp.float32)
        _ctx_2048c = jax.random.dirichlet(jax.random.fold_in(_rk, 512), 0.3 * jnp.ones((16,), jnp.float32), (16, 128))
        _ctx_2048t = jnp.einsum('bsk,bkd->bsd', _ctx_2048c, _ctx_2048P)
        _ctx_2048t = _ctx_2048t * jax.lax.rsqrt(jnp.mean(jnp.square(_ctx_2048t)) + 1e-12) * 0.953939
        ctx_2048 = 0.000675642 + 1.00031 * (_ctx_2048t + 0.3 * jax.random.normal(jax.random.fold_in(_rk, 612), (16, 128, 256), jnp.float32))
        return (x, fside_S2_0, ctx_2048)
    x, fside_S2_0, ctx_2048 = _rec_inputs()

    def _L0_attn_setup():
        import jax, jax.numpy as jnp
        import numpy as np
        N_HEADS = 16

        def _rope_tables(seq_len, head_dim, dtype=jnp.float32):
            pos = jnp.arange(seq_len, dtype=jnp.float32)[:, None]
            exps = -jnp.arange(0, head_dim, 2, dtype=jnp.float32) / head_dim
            thetas = jnp.repeat(jnp.power(10000.0, exps), 2)
            angles = pos * thetas[None, :]
            return (jnp.cos(angles).astype(dtype), jnp.sin(angles).astype(dtype))

        def _apply_rope(x, cos, sin):
            x_even = x[..., 0::2]
            x_odd = x[..., 1::2]
            x_rot = jnp.stack((-x_odd, x_even), axis=-1).reshape(x.shape)
            return x * cos[None, :, None, :] + x_rot * sin[None, :, None, :]
        key = jax.random.key(seed)
        ks = jax.random.split(key, 5)
        B, S, E = (2, 256, 256)
        scale = 1.0 / np.sqrt(E)
        return {'x': jax.random.normal(ks[0], (B, S, E), dtype=jnp.float32), 'Wq': jax.random.normal(ks[1], (E, E), dtype=jnp.float32) * scale, 'bq': jnp.zeros((E,), dtype=jnp.float32), 'Wk': jax.random.normal(ks[2], (E, E), dtype=jnp.float32) * scale, 'bk': jnp.zeros((E,), dtype=jnp.float32), 'Wv': jax.random.normal(ks[3], (E, E), dtype=jnp.float32) * scale, 'bv': jnp.zeros((E,), dtype=jnp.float32), 'Wo': jax.random.normal(ks[4], (E, E), dtype=jnp.float32) * scale, 'bo': jnp.zeros((E,), dtype=jnp.float32)}
    _L0_attn_all = _L0_attn_setup()
    _L0_attn_in = {k: v for k, v in _L0_attn_all.items() if k in ('Wq', 'bq', 'Wk', 'bk', 'Wv', 'bv', 'Wo', 'bo')}
    del _L0_attn_all

    def _L0_xattn_setup():
        import jax, jax.numpy as jnp
        import numpy as np
        key = jax.random.key(seed)
        ks = jax.random.split(key, 5)
        B, D, L, NH = (2, 128, 256, 8)
        H = D // NH
        return {'v': jax.random.normal(ks[0], (B, D, L), jnp.float32), 'k': jax.random.normal(ks[1], (H, L), jnp.float32) * 0.1, 'bias': jax.random.normal(ks[2], (D,), jnp.float32), 'x1': jax.random.normal(ks[3], (B, D, L), jnp.float32), 'x2': jax.random.normal(ks[4], (B, D, L), jnp.float32), 'num_heads': NH}
    _L0_xattn_all = _L0_xattn_setup()
    _L0_xattn_in = {k: v for k, v in _L0_xattn_all.items() if k in ('k',)}
    del _L0_xattn_all

    def _L0_ffn_setup():
        import jax, jax.numpy as jnp
        import numpy as np
        B, S, H = (4, 128, 256)
        E, K, I, SI = (16, 4, 176, 704)

        def _silu_mul(gu, inter):
            return jax.nn.silu(gu[:, :inter]) * gu[:, inter:]
        key = jax.random.key(seed)
        ks = jax.random.split(key, 7)
        s = 0.02
        return {'hidden_states': jax.random.normal(ks[0], (B, S, H), jnp.float32), 'gate_w': jax.random.normal(ks[1], (E, H), jnp.float32) * s, 'expert_gate_up': jax.random.normal(ks[2], (E, 2 * I, H), jnp.float32) * s, 'expert_down': jax.random.normal(ks[3], (E, H, I), jnp.float32) * s, 'shared_gate_up': jax.random.normal(ks[4], (2 * SI, H), jnp.float32) * s, 'shared_down': jax.random.normal(ks[5], (H, SI), jnp.float32) * s, 'shared_gate_vec': jax.random.normal(ks[6], (1, H), jnp.float32) * s}
    _L0_ffn_all = _L0_ffn_setup()
    _L0_ffn_in = {k: v for k, v in _L0_ffn_all.items() if k in ('gate_w', 'expert_gate_up', 'expert_down', 'shared_gate_up', 'shared_down', 'shared_gate_vec')}
    del _L0_ffn_all
    return {'x': x, 'fside_S2_0': fside_S2_0, 'ctx_2048': ctx_2048, 'L0_attn_Wq': _L0_attn_in['Wq'], 'L0_attn_bq': _L0_attn_in['bq'], 'L0_attn_Wk': _L0_attn_in['Wk'], 'L0_attn_bk': _L0_attn_in['bk'], 'L0_attn_Wv': _L0_attn_in['Wv'], 'L0_attn_bv': _L0_attn_in['bv'], 'L0_attn_Wo': _L0_attn_in['Wo'], 'L0_attn_bo': _L0_attn_in['bo'], 'L0_xattn_k': _L0_xattn_in['k'], 'L0_ffn_gate_w': _L0_ffn_in['gate_w'], 'L0_ffn_expert_gate_up': _L0_ffn_in['expert_gate_up'], 'L0_ffn_expert_down': _L0_ffn_in['expert_down'], 'L0_ffn_shared_gate_up': _L0_ffn_in['shared_gate_up'], 'L0_ffn_shared_down': _L0_ffn_in['shared_down'], 'L0_ffn_shared_gate_vec': _L0_ffn_in['shared_gate_vec']}

def reference(x, fside_S2_0, ctx_2048, L0_attn_Wq, L0_attn_bq, L0_attn_Wk, L0_attn_bk, L0_attn_Wv, L0_attn_bv, L0_attn_Wo, L0_attn_bo, L0_xattn_k, L0_ffn_gate_w, L0_ffn_expert_gate_up, L0_ffn_expert_down, L0_ffn_shared_gate_up, L0_ffn_shared_down, L0_ffn_shared_gate_vec):
    import jax
    import jax.numpy as jnp

    def _L0_attn_ref(x, Wq, bq, Wk, bk, Wv, bv, Wo, bo):
        import jax, jax.numpy as jnp
        import numpy as np
        N_HEADS = 16

        def _rope_tables(seq_len, head_dim, dtype=jnp.float32):
            pos = jnp.arange(seq_len, dtype=jnp.float32)[:, None]
            exps = -jnp.arange(0, head_dim, 2, dtype=jnp.float32) / head_dim
            thetas = jnp.repeat(jnp.power(10000.0, exps), 2)
            angles = pos * thetas[None, :]
            return (jnp.cos(angles).astype(dtype), jnp.sin(angles).astype(dtype))

        def _apply_rope(x, cos, sin):
            x_even = x[..., 0::2]
            x_odd = x[..., 1::2]
            x_rot = jnp.stack((-x_odd, x_even), axis=-1).reshape(x.shape)
            return x * cos[None, :, None, :] + x_rot * sin[None, :, None, :]
        B, S, E = x.shape
        H = N_HEADS
        D = E // H
        cos, sin = _rope_tables(S, D, x.dtype)
        q = (x @ Wq + bq).reshape(B, S, H, D)
        k = (x @ Wk + bk).reshape(B, S, H, D)
        v = (x @ Wv + bv).reshape(B, S, H, D)
        q = _apply_rope(q, cos, sin)
        k = _apply_rope(k, cos, sin)
        scores = jnp.einsum('bshd,bthd->bhst', q, k) / jnp.sqrt(jnp.asarray(D, x.dtype))
        causal = jnp.triu(jnp.ones((S, S), dtype=bool), k=1)
        scores = jnp.where(causal[None, None], -jnp.inf, scores)
        attn = jax.nn.softmax(scores, axis=-1)
        out = jnp.einsum('bhst,bthd->bshd', attn, v).reshape(B, S, E)
        return out @ Wo + bo

    def _L0_xattn_ref(v, k, bias, x1, x2, num_heads):
        import jax, jax.numpy as jnp
        import numpy as np
        B, D, L = v.shape
        H = D // num_heads
        fft_size = 2 * L
        vr = v.reshape(B, H, num_heads, L)
        x1r = x1.reshape(B, H, num_heads, L)
        x2r = x2.reshape(B, H, num_heads, L)
        kv = vr[:, :, :, None, :] * x2r[:, :, None, :, :]
        k_f = jnp.fft.rfft(k.astype(jnp.float32), n=fft_size)
        y = jnp.fft.irfft(jnp.fft.rfft(kv, n=fft_size) * k_f[None, :, None, None, :], n=fft_size)[..., :L]
        skip = bias.astype(jnp.float32).reshape(H, num_heads)[None, :, :, None, None]
        y = y + kv * skip
        out = jnp.einsum('bhijl,bhil->bhjl', y, x1r)
        return out.reshape(B, D, L)

    def _L0_ffn_ref(hidden_states, gate_w, expert_gate_up, expert_down, shared_gate_up, shared_down, shared_gate_vec):
        import jax, jax.numpy as jnp
        import numpy as np
        B, S, H = (4, 128, 256)
        E, K, I, SI = (16, 4, 176, 704)

        def _silu_mul(gu, inter):
            return jax.nn.silu(gu[:, :inter]) * gu[:, inter:]
        orig_shape = hidden_states.shape
        x = hidden_states.reshape(-1, H)
        router_logits = x @ gate_w.T
        routing_probs = jax.nn.softmax(router_logits.astype(jnp.float32), axis=-1)
        topk_w, topk_idx = jax.lax.top_k(routing_probs, K)
        topk_w = topk_w / topk_w.sum(axis=-1, keepdims=True)
        topk_w = topk_w.astype(x.dtype)
        combine = (jax.nn.one_hot(topk_idx, E, dtype=x.dtype) * topk_w[..., None]).sum(1)
        shared = _silu_mul(x @ shared_gate_up.T, SI) @ shared_down.T
        shared = shared * jax.nn.sigmoid(x @ shared_gate_vec.T)

        def step(acc, ew):
            w_gu, w_d, cw = ew
            h = _silu_mul(x @ w_gu.T, I)
            return (acc + h @ w_d.T * cw[:, None], None)
        acc0 = jnp.zeros_like(x)
        sparse, _ = jax.lax.scan(step, acc0, (expert_gate_up, expert_down, combine.T))
        return (shared + sparse).reshape(orig_shape)
    x = x + _L0_attn_ref(_layernorm(x, axis=-1), L0_attn_Wq, L0_attn_bq, L0_attn_Wk, L0_attn_bk, L0_attn_Wv, L0_attn_bv, L0_attn_Wo, L0_attn_bo)
    x = x + _L0_xattn_ref(_layernorm(x, axis=-1), L0_xattn_k, fside_S2_0, ctx_2048, ctx_2048, 8)
    x = x + _L0_ffn_ref(_layernorm(x, axis=-1), L0_ffn_gate_w, L0_ffn_expert_gate_up, L0_ffn_expert_down, L0_ffn_shared_gate_up, L0_ffn_shared_down, L0_ffn_shared_gate_vec)
    return x

_drawn_inputs = setup_inputs


def setup_inputs(seed=0):
    import zlib

    import numpy as np

    out = dict(_drawn_inputs(seed))
    spreads = {'L0_attn_bq': (0.0, 0.36),
     'L0_attn_bk': (0.0, 0.695),
     'L0_attn_bv': (0.0, 0.1),
     'L0_attn_bo': (0.0, 0.1)}
    factors = {'L0_ffn_gate_w': 8.0,
     'L0_ffn_expert_gate_up': 8.0,
     'L0_ffn_expert_down': 8.0,
     'L0_ffn_shared_gate_up': 8.0,
     'L0_ffn_shared_down': 8.0,
     'L0_ffn_shared_gate_vec': 8.0}
    for name, (base, spread) in spreads.items():
        noise = np.random.default_rng([zlib.crc32(name.encode()), seed]).standard_normal(out[name].shape)
        drawn = base * np.exp(spread * noise) if base else spread * noise
        out[name] = jnp.asarray(drawn.astype(out[name].dtype))
    for name, factor in factors.items():
        out[name] = (out[name] * factor).astype(out[name].dtype)
    return out
```

```python
from contextlib import ExitStack

import numpy as np
import concourse.bass as bass
from concourse import mybir

ALU = mybir.AluOpType
ACT = mybir.ActivationFunctionType
F32 = mybir.dt.float32
F16 = mybir.dt.float16
X = mybir.AxisListType.X

P = 128
E = 256
KC = E // P
HEADS, HD = 16, 16
GROUPS, SIDE = 16, 8
EXPERTS, TOP, INTER, SHARED = 16, 4, 176, 704
CHUNK = 2 * INTER
NCHUNK = (EXPERTS * INTER + SHARED) // CHUNK
NSPARSE = EXPERTS * INTER // CHUNK
DT = 3
DPAD = DT * P
WS = 64.0
EPS = 1e-5
NEG = -1e30
QK, V0, O0, R0, NR = 8 * P, 8 * P, 8 * P + E, 8 * P + 2 * E, EXPERTS + 1
AW = R0 + 20
GU = KC * 2 * CHUNK
STAGE = GU + DT * E


class Row:

    def __init__(self, b, half, par):
        self.b, self.half, self.par = b, half, par


def numbered(b):
    return Row(b, b // 2, b % 2)


class Signal:

    def __init__(self, sem, per):
        self.sem, self.per = sem, per

    def value(self, row, k=None, back=0):
        k = self.per if k is None else k
        return row.b * self.per + (k - back * self.per)

    def wait(self, eng, row, k=None, back=0):
        if isinstance(row.b, int) and row.b < back:
            return
        eng.wait_ge(self.sem, self.value(row, k, back))


def build(nc, x, ctx_in, w_attn, w_moe, toep, bias_qk, bias_v, bias_o, skip,
          trig, causal, ident, halves, out):
    NB = x.shape[0]
    stack = ExitStack()
    with stack:
        def sb(name, shape, dt=F32):
            return stack.enter_context(nc.sbuf_tensor(name, shape, dt))

        def sem(name):
            return stack.enter_context(nc.semaphore(name))

        def signal(name, per=1):
            return Signal(sem(name), per)

        wa = [sb(f"w_attn_{n}", [P, KC, AW], F16) for n in ("hi", "lo")]
        wgu = [sb(f"w_gate_up_{n}", [P, NCHUNK, KC, 2, CHUNK], F16) for n in ("hi", "lo")]
        wd = [sb(f"w_down_{n}", [P, NCHUNK, DT, E], F16) for n in ("hi", "lo")]
        toep_sb = sb("toeplitz", [P, GROUPS, 2, P])
        bqk_sb = sb("bias_qk_sb", [P, 8])
        bv_sb = sb("bias_v_sb", [P, E])
        bo_sb = sb("bias_o_sb", [P, E])
        skip_sb = sb("skip_sb", [P, P])
        trig_sb = sb("trig_sb", [P, 2, P])
        causal_sb = sb("causal_sb", [P, P])
        id_sb = sb("identity", [P, P])
        halves_sb = sb("halves_sb", [P, 2])
        stage = [sb(f"stage_moe{i}", [P, STAGE]) for i in range(2)]
        x_sb = [sb(f"x_sb{i}", [P, E]) for i in range(2)]
        c_sb = [sb(f"ctx_sb{i}", [P, E]) for i in range(2)]
        xb = sb("x_plus_bias", [P, E])
        st6 = sb("ln_stats", [P, 6])
        mv = sb("ln_mean_var", [P, 2])
        var = sb("ln_var", [P, 1])
        rstd = sb("ln_rstd", [P, 1])
        minus_half = sb("minus_half", [P, 1])
        xn = sb("x_norm", [P, E])
        tT = [sb(f"lhs_t_{n}", [P, KC, P], F16) for n in ("hi", "lo")]
        qkb = sb("qk_biased", [P, 8, P])
        rc = sb("rope_cos", [P, 2, 2, P])
        rs = sb("rope_sin", [P, 2, 2, P])
        qk = sb("qk_roped", [P, 2, 2, P])
        kmask = sb("k_by_parity", [P, 2, KC, P])
        v_sb = sb("v_sb", [P, HEADS, HD + 1])
        both = sb("scores_and_probs_t", [P, 2, 4, 4, P])
        sm, pT = both[:, 0], both[:, 1]
        stage_a = both[:].rearrange("p a g s n -> p (a g s n)")[:, 0:KC * AW]
        mx = sb("row_max", [P, 4, 4])
        rsum = sb("softmax_recip", [P, HEADS])
        o_sb = sb("attn_out", [P, E])
        x1 = sb("x1", [P, E])
        vcT = sb("v_ctx_t", [P, 2, KC, P])
        kv = sb("kv", [P, KC, GROUPS, SIDE * SIDE])
        sk1 = sb("skip_prod", [P, KC, P])
        sk2 = sb("skip_scaled", [P, KC, P])
        sks = sb("skip_sum", [P, KC, GROUPS])
        skc = sb("skip_out", [P, KC, P])
        z = sb("conv_gated", [P, 2 * 512])
        o2 = sb("conv_sum", [P, KC, P])
        o2f = sb("conv_out", [P, KC, P])
        x2 = [sb(f"x2_{i}", [P, E]) for i in range(2)]
        xT = [[sb(f"moe_x_t{i}_{n}", [P, KC, P], F16) for n in ("hi", "lo")] for i in range(2)]
        lg = sb("logits", [P, EXPERTS + 8 - TOP])
        top8 = sb("top8", [P, 8])
        picks = sb("picks", [P, 8])
        picked = sb("picked", [P, EXPERTS + 8 - TOP])
        lmax = sb("logit_neg_max", [P, 1])
        ex = sb("router_exp", [P, EXPERTS])
        gth = sb("gate_tanh", [P, 1])
        esel = sb("router_sel", [P, EXPERTS])
        esum = sb("router_sum", [P, 1])
        erec = sb("router_recip", [P, 1])
        cw = [sb(f"expert_weight{i}", [P, NR]) for i in range(2)]
        th = sb("gate_act", [P, CHUNK])
        ga = sb("gate_prod", [P, CHUNK])
        hh = sb("inner", [P, DPAD])
        hT = [sb(f"inner_t_{n}", [P, DT, P], F16) for n in ("hi", "lo")]
        y_sb = [sb(f"y_sb{i}", [P, E]) for i in range(2)]

        def bank(name):
            return stack.enter_context(nc.psum_tensor(name, [P, 512], F32))

        pg, pu, ph, pacc = bank("ps_gate"), bank("ps_up"), bank("ps_inner_t"), bank("ps_out")
        pf = stack.enter_context(nc.psum_tensor("ps_front", [P, 4, 512], F32))

        s_const = sem("const_loaded")
        s_wa = sem("attn_weights_loaded")
        s_toep = sem("toeplitz_loaded")
        s_stage = [sem(f"moe_weights_loaded{i}") for i in range(2)]
        s_x = [sem(f"x_loaded{i}") for i in range(2)]
        s_c = [sem(f"ctx_loaded{i}") for i in range(2)]
        s_y = [sem(f"y_stored{i}") for i in range(2)]
        s_wa_hi, s_wa_lo = sem("attn_hi_done"), sem("attn_lo_done")
        s_w_hi, s_w_lo = sem("moe_hi_done"), sem("moe_lo_done")
        s_once = sem("constants_set")
        s_half = sem("minus_half_set")

        ln_step = signal("ln_step", 9)
        rstd_ready = signal("rstd_ready", 3)
        normed = signal("normed", 3)
        xb_ready = signal("x_plus_bias_ready")
        xn_T = signal("xn_transposed")
        lhs_hi = signal("lhs_hi", 2)
        lhs_lo = signal("lhs_lo", 2)
        q_ready = signal("q_projected")
        k_ready = signal("k_projected")
        v_ready = signal("v_projected")
        qk_biased = signal("qk_biased", 2)
        v_done = signal("v_done")
        cos_done = signal("cos_done", 2)
        sin_done = signal("sin_done", 2)
        roped = signal("roped", 2)
        k_masked = signal("k_masked")
        scored = signal("scored")
        masked = signal("masked", 4)
        maxed = signal("maxed", 4)
        shifted = signal("shifted", 4)
        exped = signal("exped", 4)
        probs_T = signal("probs_transposed", 4)
        pT_ready = signal("probs_t_ready", 4)
        av_ready = signal("av_ready")
        recip_done = signal("recip_done")
        o_ready = signal("attn_out_ready")
        o_T = signal("attn_out_transposed")
        wo_ready = signal("wo_ready")
        x1_ready = signal("x1_ready")
        vc_T = signal("v_ctx_transposed")
        vc_ready = signal("v_ctx_ready")
        kv_ready = signal("kv_ready", 2)
        sk_mul = signal("skip_multiplied", 2)
        sk_sum = signal("skip_summed")
        sk_out = signal("skip_out_done")
        conv_ready = signal("conv_ready", 2)
        gated = signal("conv_gated", 4)
        gsum = signal("conv_summed", 4)
        o2_ready = signal("conv_out_ready")
        o2_T = signal("conv_out_transposed")
        x2_ready = signal("x2_ready")
        xn3_T = signal("xn3_transposed")
        xT_hi = signal("moe_x_hi")
        xT_lo = signal("moe_x_lo")
        routed = signal("router_logits")
        lg_ready = signal("logits_ready")
        lmax_ready = signal("logit_max_ready")
        ex_ready = signal("router_exp_ready", 2)
        top_ready = signal("top8_ready")
        pick_done = signal("pick_done", 2)
        sel_done = signal("select_done", 3)
        cw_ready = signal("expert_weight_ready", 2)

        NC = NCHUNK
        gate_ready = signal("gate_ready", NC)
        up_ready = signal("up_ready", NC)
        tanh_done = signal("tanh_done", NC)
        gate_done = signal("gate_done", NC)
        inner_done = signal("inner_done", NC)
        inner_T = signal("inner_transposed", NC)
        inner_hi = signal("inner_hi", NC)
        inner_lo = signal("inner_lo", NC)
        down_done = signal("down_done", NC)
        y_ready = signal("y_ready")

        ring = lambda g: pf[:, g, :]

        def products(first, last):
            terms = ((0, 0), (0, 1), (1, 0))
            return [(a, b, first and n == 0, last and n == 2) for n, (a, b) in enumerate(terms)]


        def step(eng, front, moe, front_pieces, gate, turn, up, down, finish):
            for c in range(NC + 1):
                if moe is not None:
                    if c < NC:
                        gate(eng, moe, c)
                    if c > 0:
                        turn(eng, moe, c - 1)
                    if c < NC:
                        up(eng, moe, c)
                if front is not None and c < NC:
                    for piece in front_pieces.get(2 * c, ()):
                        piece(eng, front)
                if moe is not None and c > 0:
                    down(eng, moe, c - 1)
                if front is not None and c < NC:
                    for piece in front_pieces.get(2 * c + 1, ()):
                        piece(eng, front)
                if front is not None and c == NC:
                    for piece in front_pieces.get(2 * NC, ()):
                        piece(eng, front)
            if moe is not None:
                finish(eng, moe)

        def steps(eng, *fns, prepare=None):
            front_pieces = fns[0]
            none = lambda *a: None
            if prepare is not None:
                prep = lambda eng, row, c: prepare(eng, c)
                step(eng, numbered(0), numbered(0), front_pieces, prep, none, none, none, none)
            else:
                step(eng, numbered(0), None, *fns)
            step(eng, numbered(1), numbered(0), *fns)
            with eng.Fori(0, (NB - 2) // 2) as i:
                step(eng, Row(2 * i + 2, i + 1, 0), Row(2 * i + 1, i, 1), *fns)
                step(eng, Row(2 * i + 3, i + 1, 1), Row(2 * i + 2, i + 1, 0), *fns)
            step(eng, None, numbered(NB - 1), *fns)

        NCONST = 16 * 8

        def wait_apart(eng, *waits):
            values = [v if isinstance(v, int) else eng.to_reg(v) for _, v in waits]
            eng.wait_ge(s_const, NCONST)
            for (semaphore, _), value in zip(waits, values):
                eng.wait_ge(semaphore, value)

        none = lambda *a: None
        block = stack.enter_context(nc.Block())

        @block.sync
        def _(sp):
            def load_row(row):
                if not (isinstance(row.b, int) and row.b < 2):
                    wait_apart(sp, (normed.sem, normed.value(row, 1, back=2)),
                               (xb_ready.sem, xb_ready.value(row, back=2)))
                sp.dma_start(x_sb[row.par][:], x[row.b]).then_inc(s_x[row.par], 16)
                if not (isinstance(row.b, int) and row.b < 2):
                    wait_apart(sp, (vc_T.sem, vc_T.value(row, back=2)))
                sp.dma_start(c_sb[row.par][:], ctx_in[row.b]).then_inc(s_c[row.par], 16)

            def store_row(row):
                wait_apart(sp, (y_ready.sem, y_ready.value(row)))
                sp.dma_start(out[row.b], y_sb[row.par][:]).then_inc(s_y[row.par], 16)

            for dst, src in ((id_sb, ident), (bqk_sb, bias_qk), (trig_sb, trig), (causal_sb, causal),
                             (halves_sb, halves)):
                sp.dma_start(dst[:], src).then_inc(s_const, 16)
            for dst, src in ((bv_sb, bias_v), (bo_sb, bias_o), (skip_sb, skip)):
                sp.dma_start(dst[:], src.partition_broadcast(P)).then_inc(s_const, 16)
            sp.dma_start(stage_a, w_attn).then_inc(s_wa, 16)
            load_row(numbered(0))
            load_row(numbered(1))
            sp.dma_start(toep_sb[:], toep).then_inc(s_toep, 16)
            for c in range(NC):
                if c >= 2:
                    sp.wait_ge(s_w_lo, 2 * (c - 1))
                sp.dma_start(stage[c % 2][:], w_moe[c]).then_inc(s_stage[c % 2], 16)
            load_row(numbered(2))
            store_row(numbered(0))
            load_row(numbered(3))
            store_row(numbered(1))
            with sp.Fori(0, (NB - 4) // 2) as i:
                load_row(Row(2 * i + 4, i + 2, 0))
                store_row(Row(2 * i + 2, i + 1, 0))
                load_row(Row(2 * i + 5, i + 2, 1))
                store_row(Row(2 * i + 3, i + 1, 1))
            store_row(numbered(NB - 2))
            store_row(numbered(NB - 1))
            for par in range(2):
                sp.wait_ge(s_y[par], 16 * (NB // 2))

        @block.tensor
        def _(pe):
            def t_norm(pe, row):
                normed.wait(pe, row, 1)
                x2_ready.wait(pe, row, back=1)
                for c in range(KC):
                    last = nc.tensor.transpose(ring(0)[:, c * P:(c + 1) * P], xn[:, c * P:(c + 1) * P], id_sb[:])
                last.then_inc(xn_T.sem, 1)

            def projections(pe, row):
                lhs_hi.wait(pe, row, 1)
                lhs_lo.wait(pe, row, 1)
                xT_lo.wait(pe, row, back=1)
                lg_ready.wait(pe, row, back=1)
                ex_ready.wait(pe, row, back=1)
                gated.wait(pe, row, back=1)
                for side, ready in ((0, q_ready), (1, k_ready)):
                    for t in range(4):
                        col = (4 * side + t) * P
                        for kc in range(KC):
                            for a, b, first, end in products(kc == 0, kc == KC - 1):
                                last = nc.tensor.matmul(ring(1 + side)[:, t * P:(t + 1) * P],
                                                        wa[a][:, kc, col:col + P], tT[b][:, kc, :],
                                                        start=first, stop=end)
                    last.then_inc(ready.sem, 1)
                for kc in range(KC):
                    for a, b, first, end in products(kc == 0, kc == KC - 1):
                        last = nc.tensor.matmul(ring(3)[:, 0:E], tT[a][:, kc, :], wa[b][:, kc, V0:V0 + E],
                                                start=first, stop=end)
                last.then_inc(v_ready.sem, 1)

            def scores(pe, row):
                roped.wait(pe, row)
                k_masked.wait(pe, row)
                qk_biased.wait(pe, row)
                v_done.wait(pe, row)
                for c in range(KC):
                    for e in range(2):
                        for g in range(4):
                            rows = slice(32 * g, 32 * g + 32)
                            s = 2 * c + e
                            last = nc.tensor.matmul(ring(g)[:, s * P:(s + 1) * P], qk[rows, 0, c, :],
                                                    kmask[rows, e, c, :], start=True, stop=True)
                last.then_inc(scored.sem, 1)

            def t_probs(g):
                def piece(pe, row):
                    exped.wait(pe, row, g + 1)
                    for s in range(4):
                        last = nc.tensor.transpose(ring(g)[:, s * P:(s + 1) * P], sm[:, g, s, :], id_sb[:])
                    last.then_inc(probs_T.sem, 1)
                return piece

            def attend(pe, row):
                pT_ready.wait(pe, row)
                v_done.wait(pe, row)
                for h in range(HEADS):
                    g, s = (h % 8) // 2, 2 * (h // 8) + h % 2
                    last = nc.tensor.matmul(ring(0)[:, h * 17:h * 17 + 17], pT[:, g, s, :], v_sb[:, h, :],
                                            start=True, stop=True)
                last.then_inc(av_ready.sem, 1)

            def t_attn(pe, row):
                o_ready.wait(pe, row)
                for c in range(KC):
                    last = nc.tensor.transpose(ring(1)[:, c * P:(c + 1) * P], o_sb[:, c * P:(c + 1) * P], id_sb[:])
                last.then_inc(o_T.sem, 1)

            def out_proj(pe, row):
                lhs_hi.wait(pe, row, 2)
                lhs_lo.wait(pe, row, 2)
                for kc in range(KC):
                    for a, b, first, end in products(kc == 0, kc == KC - 1):
                        last = nc.tensor.matmul(ring(2)[:, 0:E], tT[a][:, kc, :], wa[b][:, kc, O0:O0 + E],
                                                start=first, stop=end)
                last.then_inc(wo_ready.sem, 1)

            def t_vc(pe, row):
                normed.wait(pe, row, 2)
                pe.wait_ge(s_c[row.par], row.half * 16 + 16)
                for n, src in ((0, xn), (1, c_sb[row.par])):
                    for c in range(KC):
                        at = (2 * n + c) * P
                        last = nc.tensor.transpose(ring(3)[:, at:at + P], src[:, c * P:(c + 1) * P], id_sb[:])
                last.then_inc(vc_T.sem, 1)

            def conv(half):
                def piece(pe, row):
                    kv_ready.wait(pe, row, half + 1)
                    if half == 0:
                        x1_ready.wait(pe, row)
                        vc_ready.wait(pe, row)
                        if isinstance(row.b, int) and row.b == 0:
                            pe.wait_ge(s_toep, 16)
                    for h in range(8 * half, 8 * half + 8):
                        to = ring(h // 4)[:, (h % 4) * P:(h % 4) * P + P]
                        nc.tensor.matmul(to.rearrange("p (c n) -> p c n", c=2), toep_sb[:, h, 0, :],
                                         kv[:, :, h, :], start=True, stop=False, skip_group_check=True)
                        last = nc.tensor.matmul(to[:, 64:128], toep_sb[:, h, 1, :], kv[:, 0, h, :],
                                                start=False, stop=True, skip_group_check=True)
                    last.then_inc(conv_ready.sem, 1)
                return piece

            def t_conv(pe, row):
                o2_ready.wait(pe, row)
                gated.wait(pe, row)
                for c in range(KC):
                    last = nc.tensor.transpose(ring(0)[:, c * P:(c + 1) * P], o2f[:, c, :], id_sb[:])
                last.then_inc(o2_T.sem, 1)

            def t_norm3(pe, row):
                normed.wait(pe, row, 3)
                for c in range(KC):
                    last = nc.tensor.transpose(ring(1)[:, c * P:(c + 1) * P], xn[:, c * P:(c + 1) * P], id_sb[:])
                last.then_inc(xn3_T.sem, 1)

            def router(pe, row):
                xT_hi.wait(pe, row)
                xT_lo.wait(pe, row)
                n = 0
                for kc in range(KC):
                    for a in range(2):
                        for b in range(2):
                            last = nc.tensor.matmul(ring(2)[:, 0:NR], xT[row.par][a][:, kc, :],
                                                    wa[b][:, kc, R0:R0 + NR], start=n == 0, stop=n == 7)
                            n += 1
                last.then_inc(routed.sem, 1)

            def half_product(bank, side, pe, row, c, ready):
                for kc in range(KC):
                    for a, b, first, end in products(kc == 0, kc == KC - 1):
                        last = nc.tensor.matmul(bank[:, 0:CHUNK], xT[row.par][a][:, kc, :],
                                                wgu[b][:, c, kc, side, :], start=first, stop=end)
                last.then_inc(ready.sem, 1)

            def gate(pe, row, c):
                if c == 0:
                    xT_hi.wait(pe, row)
                    xT_lo.wait(pe, row)
                    gate_done.wait(pe, row, back=1)
                else:
                    gate_done.wait(pe, row, c)
                if isinstance(row.b, int) and row.b == 0:
                    pe.wait_ge(s_w_lo, 2 * c + 2)
                    pe.wait_ge(s_w_hi, 2 * c + 2)
                half_product(pg, 0, pe, row, c, gate_ready)

            def up(pe, row, c):
                if c == 0:
                    inner_done.wait(pe, row, back=1)
                else:
                    inner_done.wait(pe, row, c)
                half_product(pu, 1, pe, row, c, up_ready)

            def turn(pe, row, c):
                inner_done.wait(pe, row, c + 1)
                if c == 0:
                    inner_lo.wait(pe, row, back=1)
                else:
                    inner_lo.wait(pe, row, c)
                for t in range(DT):
                    last = nc.tensor.transpose(ph[:, t * P:(t + 1) * P], hh[:, t * P:(t + 1) * P], id_sb[:])
                last.then_inc(inner_T.sem, 1)

            def down(pe, row, c):
                inner_hi.wait(pe, row, c + 1)
                inner_lo.wait(pe, row, c + 1)
                if c == 0:
                    y_ready.wait(pe, row, back=1)
                for t in range(DT):
                    for a, b, first, end in products(c == 0 and t == 0, c == NC - 1 and t == DT - 1):
                        last = nc.tensor.matmul(pacc[:, 0:E], hT[a][:, t, :], wd[b][:, c, t, :],
                                                start=first, stop=end)
                last.then_inc(down_done.sem, 1)

            pe.wait_ge(s_const, NCONST)
            pe.wait_ge(s_wa_lo, 1)
            pe.wait_ge(s_once, 4)
            pieces = {1: [t_norm], 3: [projections], 5: [scores], 8: [t_probs(0), t_probs(1)],
                      9: [t_probs(2), t_probs(3)], 10: [attend], 11: [t_attn], 12: [out_proj],
                      13: [t_vc], 15: [conv(0)], 16: [conv(1)], 18: [t_conv], 19: [t_norm3], 20: [router]}
            steps(pe, pieces, gate, turn, up, down, none)

        @block.scalar
        def _(act):
            def lhs_split(n):
                def piece(act, row):
                    (xn_T, o_T)[n].wait(act, row)
                    if n == 0:
                        wo_ready.wait(act, row, back=1)
                    else:
                        v_ready.wait(act, row)
                    nc.scalar.activation(tT[0][:].rearrange("p c n -> p (c n)"), ring(n)[:, 0:E],
                                         ACT.Copy).then_inc(lhs_hi.sem, 1)
                return piece

            def biased(side):
                def piece(act, row):
                    (q_ready, k_ready)[side].wait(act, row)
                    cos_done.wait(act, row, back=1)
                    sin_done.wait(act, row, back=1)
                    for t in range(4):
                        n = 4 * side + t
                        last = nc.scalar.activation(qkb[:, n, :], ring(1 + side)[:, t * P:(t + 1) * P],
                                                    ACT.Identity, bias=bqk_sb[:, n:n + 1], scale=1.0 / WS)
                    last.then_inc(qk_biased.sem, 1)
                return piece

            def exp_probs(g):
                def piece(act, row):
                    shifted.wait(act, row, g + 1)
                    nc.scalar.activation(sm[:, g, :, :].rearrange("p s n -> p (s n)"),
                                         sm[:, g, :, :].rearrange("p s n -> p (s n)"),
                                         ACT.Exp, scale=HD ** -0.5).then_inc(exped.sem, 1)
                return piece

            def copy_probs(g):
                def piece(act, row):
                    probs_T.wait(act, row, g + 1)
                    av_ready.wait(act, row, back=1)
                    nc.scalar.activation(pT[:, g, :, :].rearrange("p s n -> p (s n)"), ring(g),
                                         ACT.Copy).then_inc(pT_ready.sem, 1)
                return piece

            def copy_vc(act, row):
                vc_T.wait(act, row)
                gated.wait(act, row, back=1)
                o2_ready.wait(act, row, back=1)
                kv_ready.wait(act, row, back=1)
                nc.scalar.activation(vcT[:].rearrange("p a c n -> p (a c n)"), ring(3),
                                     ACT.Copy).then_inc(vc_ready.sem, 1)

            def moe_x_hi(act, row):
                xn3_T.wait(act, row)
                if not (isinstance(row.b, int) and row.b < 2):
                    up_ready.wait(act, row, back=2)
                nc.scalar.activation(xT[row.par][0][:].rearrange("p c n -> p (c n)"), ring(1)[:, 0:E],
                                     ACT.Copy).then_inc(xT_hi.sem, 1)

            def router_exp(act, row):
                lmax_ready.wait(act, row)
                sel_done.wait(act, row, back=1)
                cw_ready.wait(act, row, back=1)
                nc.scalar.activation(ex[:], lg[:, 0:EXPERTS], ACT.Exp, bias=lmax[:]).then_inc(ex_ready.sem, 1)
                nc.scalar.activation(gth[:], ring(2)[:, EXPERTS:NR], ACT.Tanh, scale=0.5 / WS)\
                    .then_inc(ex_ready.sem, 1)

            def gate(act, row, c):
                gate_ready.wait(act, row, c + 1)
                if c == 0:
                    gate_done.wait(act, row, back=1)
                else:
                    gate_done.wait(act, row, c)
                nc.scalar.activation(th[:], pg[:, 0:CHUNK], ACT.Tanh, scale=0.5 / WS).then_inc(tanh_done.sem, 1)

            def turn(act, row, c):
                inner_T.wait(act, row, c + 1)
                if c == 0:
                    down_done.wait(act, row, back=1)
                else:
                    down_done.wait(act, row, c)
                nc.scalar.activation(hT[0][:].rearrange("p t n -> p (t n)"), ph[:, 0:DPAD],
                                     ACT.Copy).then_inc(inner_hi.sem, 1)

            act.wait_ge(s_const, NCONST)
            act.wait_ge(s_wa, 16)
            nc.scalar.activation(wa[0][:].rearrange("p k n -> p (k n)"), stage_a, ACT.Copy,
                                 scale=WS).then_inc(s_wa_hi, 1)

            def prepare(act, c):
                act.wait_ge(s_stage[c % 2], 16 * (c // 2 + 1))
                nc.scalar.activation(wgu[0][:, c].rearrange("p k s n -> p (k s n)"), stage[c % 2][:, 0:GU],
                                     ACT.Copy, scale=WS).then_inc(s_w_hi, 1)
                nc.scalar.activation(wd[0][:, c].rearrange("p t n -> p (t n)"), stage[c % 2][:, GU:STAGE],
                                     ACT.Copy, scale=WS).then_inc(s_w_hi, 1)

            pieces = {1: [lhs_split(0)], 3: [biased(0), biased(1)], 6: [exp_probs(0), exp_probs(1)],
                      7: [exp_probs(2), exp_probs(3)], 8: [copy_probs(0), copy_probs(1)],
                      9: [copy_probs(2), copy_probs(3)], 11: [lhs_split(1)], 13: [copy_vc],
                      19: [moe_x_hi], 20: [router_exp]}
            steps(act, pieces, gate, turn, none, none, none, prepare=prepare)

        @block.vector
        def _(dve):
            def norm(n, src_of, ready):
                def piece(dve, row):
                    ready(dve, row)
                    src = src_of(row)
                    nc.vector.bn_stats(st6[:], src).then_inc(ln_step.sem, 1)
                    wait_apart(dve, (ln_step.sem, ln_step.value(row, 3 * n + 1)))
                    nc.vector.bn_aggr(mv[:], st6[:]).then_inc(ln_step.sem, 1)
                    ln_step.wait(dve, row, 3 * n + 2)
                    nc.vector.tensor_scalar(var[:], mv[:, 1:2], EPS, None, ALU.add).then_inc(ln_step.sem, 1)
                    rstd_ready.wait(dve, row, n + 1)
                    if n == 0:
                        xn3_T.wait(dve, row, back=1)
                    elif n == 1:
                        xn_T.wait(dve, row)
                    else:
                        vc_T.wait(dve, row)
                    nc.vector.tensor_scalar(xn[:], src, mv[:, 0:1], rstd[:], ALU.subtract, ALU.mult)\
                        .then_inc(normed.sem, 1)
                return piece

            norm1 = norm(0, lambda row: x_sb[row.par][:],
                         lambda dve, row: dve.wait_ge(s_x[row.par], row.half * 16 + 16))
            norm2 = norm(1, lambda row: x1[:], lambda dve, row: x1_ready.wait(dve, row))
            norm3 = norm(2, lambda row: x2[row.par][:], lambda dve, row: x2_ready.wait(dve, row))

            def lhs_split(n):
                def piece(dve, row):
                    lhs_hi.wait(dve, row, n + 1)
                    nc.vector.tensor_tensor(tT[1][:].rearrange("p c n -> p (c n)"), ring(n)[:, 0:E],
                                            tT[0][:].rearrange("p c n -> p (c n)"), ALU.subtract)\
                        .then_inc(lhs_lo.sem, 1)
                return piece

            def v_bias(dve, row):
                v_ready.wait(dve, row)
                av_ready.wait(dve, row, back=1)
                nc.vector.scalar_tensor_tensor(
                    out=v_sb[:, :, 0:HD], in0=ring(3)[:, 0:E].rearrange("p (h d) -> p h d", d=HD), scalar=1.0 / WS,
                    in1=bv_sb[:].rearrange("p (h d) -> p h d", d=HD), op0=ALU.mult, op1=ALU.add)\
                    .then_inc(v_done.sem, 1)

            def rope(side):
                def piece(dve, row):
                    qk_biased.wait(dve, row, side + 1)
                    cos = trig_sb[:, 0:1, :].broadcast_to([P, 2, P])
                    nc.vector.tensor_tensor(rc[:, side], qkb[:, 4 * side:4 * side + 2, :], cos, ALU.mult)\
                        .then_inc(cos_done.sem, 1)
                    cos_done.wait(dve, row, side + 1)
                    sin_done.wait(dve, row, side + 1)
                    scored.wait(dve, row, back=1)
                    nc.vector.tensor_tensor(qk[:, side], rc[:, side], rs[:, side], ALU.add).then_inc(roped.sem, 1)
                return piece

            def mask_max(g):
                def piece(dve, row):
                    if g == 0:
                        scored.wait(dve, row)
                        probs_T.wait(dve, row, back=1)
                        shifted.wait(dve, row, back=1)
                    nc.vector.tensor_tensor(sm[:, g], ring(g).rearrange("p (s n) -> p s n", n=P),
                                            causal_sb[:].rearrange("p (a n) -> p a n", a=1).broadcast_to([P, 4, P]),
                                            ALU.add).then_inc(masked.sem, 1)
                    masked.wait(dve, row, g + 1)
                    nc.vector.tensor_reduce(mx[:, g, :], sm[:, g], X, ALU.max).then_inc(maxed.sem, 1)
                return piece

            def normalise(dve, row):
                av_ready.wait(dve, row)
                o = ring(0)[:, 0:HEADS * 17].rearrange("p (h d) -> p h d", d=17)
                nc.vector.reciprocal(rsum[:].rearrange("p (h a) -> p h a", a=1), o[:, :, HD:HD + 1])\
                    .then_inc(recip_done.sem, 1)
                recip_done.wait(dve, row)
                o_T.wait(dve, row, back=1)
                nc.vector.tensor_tensor(o_sb[:].rearrange("p (h d) -> p h d", d=HD), o[:, :, 0:HD],
                                        rsum[:].rearrange("p (h a) -> p h a", a=1).broadcast_to([P, HEADS, HD]),
                                        ALU.mult).then_inc(o_ready.sem, 1)

            def residual1(dve, row):
                wo_ready.wait(dve, row)
                xb_ready.wait(dve, row)
                x2_ready.wait(dve, row, back=1)
                nc.vector.scalar_tensor_tensor(out=x1[:], in0=ring(2)[:, 0:E], scalar=1.0 / WS, in1=xb[:],
                                               op0=ALU.mult, op1=ALU.add).then_inc(x1_ready.sem, 1)

            def skip_sum(dve, row):
                sk_mul.wait(dve, row)
                sk_out.wait(dve, row, back=1)
                nc.vector.tensor_reduce(sks[:].rearrange("p c g -> p (c g)"),
                                        sk2[:].rearrange("p c (g i) -> p (c g) i", i=SIDE),
                                        X, ALU.add).then_inc(sk_sum.sem, 1)

            def gate_conv(half, c):
                def piece(dve, row):
                    k = 2 * half + c
                    conv_ready.wait(dve, row, half + 1)
                    if k > 0:
                        gsum.wait(dve, row, k)
                    else:
                        gsum.wait(dve, row, back=1)
                        o2_ready.wait(dve, row, back=1)
                    G2 = GROUPS // 2
                    y = pf[:, 2 * half:2 * half + 2, :].rearrange("p b (h c n) -> p (b h) c n", h=4, c=2)[:, :, c, :]
                    y = y.rearrange("p h (j i) -> p h j i", i=SIDE)
                    cT = vcT[:, 1, c, half * 64:half * 64 + 64].rearrange("p (h a i) -> p h a i", a=1, i=SIDE)
                    zz = z[:, k % 2 * 512:k % 2 * 512 + 512].rearrange("p (h j i) -> p h j i", j=SIDE, i=SIDE)
                    nc.vector.tensor_tensor(zz, y, cT.broadcast_to([P, G2, SIDE, SIDE]), ALU.mult)\
                        .then_inc(gated.sem, 1)
                    gated.wait(dve, row, k + 1)
                    nc.vector.tensor_reduce(o2[:, c, half * 64:half * 64 + 64],
                                            z[:, k % 2 * 512:k % 2 * 512 + 512].rearrange("p (n i) -> p n i", i=SIDE),
                                            X, ALU.add).then_inc(gsum.sem, 1)
                return piece

            def residual2(dve, row):
                o2_T.wait(dve, row)
                if not (isinstance(row.b, int) and row.b < 2):
                    y_ready.wait(dve, row, back=2)
                nc.vector.tensor_tensor(x2[row.par][:], ring(0)[:, 0:E], x1[:], ALU.add).then_inc(x2_ready.sem, 1)

            def moe_x_lo(dve, row):
                xT_hi.wait(dve, row)
                nc.vector.tensor_tensor(xT[row.par][1][:].rearrange("p c n -> p (c n)"), ring(1)[:, 0:E],
                                        xT[row.par][0][:].rearrange("p c n -> p (c n)"), ALU.subtract)\
                    .then_inc(xT_lo.sem, 1)

            def logits(dve, row):
                routed.wait(dve, row)
                ex_ready.wait(dve, row, back=1)
                nc.vector.tensor_scalar(lg[:, 0:EXPERTS], ring(2)[:, 0:EXPERTS], 1.0 / WS, None, ALU.mult)\
                    .then_inc(lg_ready.sem, 1)
                wait_apart(dve, (lg_ready.sem, lg_ready.value(row)))
                nc.vector.max(top8[:], lg[:, 0:EXPERTS]).then_inc(top_ready.sem, 1)
                top_ready.wait(dve, row)
                nc.vector.tensor_scalar(lmax[:], top8[:, 0:1], -1.0, None, ALU.mult).then_inc(lmax_ready.sem, 1)

            def choose(dve, row):
                k = 0.5 / (WS * WS)
                nc.vector.tensor_copy(picks[:, 0:TOP], top8[:, 0:TOP]).then_inc(pick_done.sem, 1)
                wait_apart(dve, (pick_done.sem, pick_done.value(row, 1)))
                nc.vector.match_replace(out=picked[:], in_to_replace=picks[:], in_values=lg[:], imm_value=-NEG)\
                    .then_inc(pick_done.sem, 1)
                pick_done.wait(dve, row, 2)
                ex_ready.wait(dve, row)
                nc.vector.scalar_tensor_tensor(out=esel[:], in0=picked[:, 0:EXPERTS], scalar=-NEG, in1=ex[:],
                                               op0=ALU.is_equal, op1=ALU.mult).then_inc(sel_done.sem, 1)
                sel_done.wait(dve, row, 1)
                nc.vector.reduce_sum(esum[:], esel[:], X).then_inc(sel_done.sem, 1)
                sel_done.wait(dve, row, 2)
                nc.vector.reciprocal(erec[:], esum[:]).then_inc(sel_done.sem, 1)
                sel_done.wait(dve, row, 3)
                if not (isinstance(row.b, int) and row.b < 2):
                    inner_done.wait(dve, row, back=2)
                nc.vector.tensor_scalar(cw[row.par][:, 0:EXPERTS], esel[:], erec[:], k, ALU.mult, ALU.mult)\
                    .then_inc(cw_ready.sem, 1)
                nc.vector.tensor_scalar(cw[row.par][:, EXPERTS:NR], gth[:], 1.0, 0.5 * k, ALU.add, ALU.mult)\
                    .then_inc(cw_ready.sem, 1)

            def gate(dve, row, c):
                tanh_done.wait(dve, row, c + 1)
                if c == 0:
                    inner_done.wait(dve, row, back=1)
                else:
                    inner_done.wait(dve, row, c)
                nc.vector.scalar_tensor_tensor(out=ga[:], in0=th[:], scalar=1.0, in1=pg[:, 0:CHUNK],
                                               op0=ALU.add, op1=ALU.mult).then_inc(gate_done.sem, 1)

            def turn(dve, row, c):
                inner_hi.wait(dve, row, c + 1)
                nc.vector.tensor_tensor(hT[1][:].rearrange("p t n -> p (t n)"), ph[:, 0:DPAD],
                                        hT[0][:].rearrange("p t n -> p (t n)"), ALU.subtract)\
                    .then_inc(inner_lo.sem, 1)

            def up(dve, row, c):
                gate_done.wait(dve, row, c + 1)
                up_ready.wait(dve, row, c + 1)
                if c == 0:
                    inner_T.wait(dve, row, back=1)
                    cw_ready.wait(dve, row)
                else:
                    inner_T.wait(dve, row, c)
                if c < NSPARSE:
                    for n in range(2):
                        cols = slice(n * INTER, (n + 1) * INTER)
                        last = nc.vector.scalar_tensor_tensor(
                            out=hh[:, cols], in0=pu[:, cols], scalar=cw[row.par][:, 2 * c + n:2 * c + n + 1],
                            in1=ga[:, cols], op0=ALU.mult, op1=ALU.mult)
                else:
                    last = nc.vector.scalar_tensor_tensor(
                        out=hh[:, 0:CHUNK], in0=pu[:, 0:CHUNK], scalar=cw[row.par][:, EXPERTS:NR],
                        in1=ga[:], op0=ALU.mult, op1=ALU.mult)
                last.then_inc(inner_done.sem, 1)

            def finish(dve, row):
                down_done.wait(dve, row)
                if not (isinstance(row.b, int) and row.b < 2):
                    dve.wait_ge(s_y[row.par], row.half * 16)
                nc.vector.scalar_tensor_tensor(out=y_sb[row.par][:], in0=pacc[:, 0:E], scalar=1.0 / WS,
                                               in1=x2[row.par][:], op0=ALU.mult, op1=ALU.add)\
                    .then_inc(y_ready.sem, 1)

            nc.vector.memset(v_sb[:, :, HD:HD + 1], 1.0).then_inc(s_once, 1)
            nc.vector.memset(hh[:, CHUNK:DPAD], 0.0).then_inc(s_once, 1)
            nc.vector.memset(lg[:, EXPERTS:], NEG).then_inc(s_once, 1)
            nc.vector.memset(picks[:, TOP:], NEG).then_inc(s_once, 1)
            dve.wait_ge(s_once, 4)
            dve.wait_ge(s_const, NCONST)
            dve.wait_ge(s_wa_hi, 1)
            nc.vector.scalar_tensor_tensor(out=wa[1][:].rearrange("p k n -> p (k n)"), in0=stage_a, scalar=WS,
                                           in1=wa[0][:].rearrange("p k n -> p (k n)"), op0=ALU.mult,
                                           op1=ALU.subtract).then_inc(s_wa_lo, 1)

            def prepare(dve, c):
                for n, (w, at, rearr) in enumerate(((wgu, slice(0, GU), "p k s n -> p (k s n)"),
                                                    (wd, slice(GU, STAGE), "p t n -> p (t n)"))):
                    dve.wait_ge(s_w_hi, 2 * c + n + 1)
                    nc.vector.scalar_tensor_tensor(out=w[1][:, c].rearrange(rearr), in0=stage[c % 2][:, at],
                                                   scalar=WS, in1=w[0][:, c].rearrange(rearr), op0=ALU.mult,
                                                   op1=ALU.subtract).then_inc(s_w_lo, 1)

            pieces = {0: [norm1], 1: [lhs_split(0)], 3: [rope(0), rope(1), v_bias],
                      5: [mask_max(0), mask_max(1)], 6: [mask_max(2), mask_max(3)],
                      10: [normalise], 11: [lhs_split(1)], 12: [residual1, norm2], 14: [skip_sum],
                      16: [gate_conv(0, 0), gate_conv(0, 1)], 17: [gate_conv(1, 0), gate_conv(1, 1)],
                      18: [residual2, norm3], 19: [moe_x_lo], 20: [logits, choose]}
            steps(dve, pieces, gate, turn, up, none, finish, prepare=prepare)

        @block.gpsimd
        def _(pool):
            def add_bias(pool, row):
                pool.wait_ge(s_x[row.par], row.half * 16 + 16)
                x1_ready.wait(pool, row, back=1)
                nc.gpsimd.tensor_tensor(xb[:], x_sb[row.par][:], bo_sb[:], ALU.add).then_inc(xb_ready.sem, 1)

            def rope_sin(side):
                def piece(pool, row):
                    qk_biased.wait(pool, row, side + 1)
                    roped.wait(pool, row, side + 1, back=1)
                    sin = trig_sb[:, 1:2, :].broadcast_to([P, 2, P])
                    nc.gpsimd.tensor_tensor(rs[:, side], qkb[:, 4 * side + 2:4 * side + 4, :], sin, ALU.mult)\
                        .then_inc(sin_done.sem, 1)
                return piece

            def mask_keys(pool, row):
                wait_apart(pool, (roped.sem, roped.value(row)))
                scored.wait(pool, row, back=1)
                for e in range(2):
                    last = nc.gpsimd.tensor_scalar(kmask[:, e], qk[:, 1], halves_sb[:, e:e + 1], None, ALU.mult)
                last.then_inc(k_masked.sem, 1)

            def shift(g):
                def piece(pool, row):
                    maxed.wait(pool, row, g + 1)
                    m = mx[:, g, :].rearrange("p (s a) -> p s a", a=1).broadcast_to([P, 4, P])
                    nc.gpsimd.tensor_tensor(sm[:, g], sm[:, g], m, ALU.subtract).then_inc(shifted.sem, 1)
                return piece

            def products_kv(pool, row):
                vc_ready.wait(pool, row)
                conv_ready.wait(pool, row, back=1)
                for half in range(2):
                    for c in range(KC):
                        cols = slice(half * 64, half * 64 + 64)
                        G2 = GROUPS // 2
                        vT = vcT[:, 0, c, cols].rearrange("p (h a i) -> p h a i", a=1, i=SIDE)
                        cT = vcT[:, 1, c, cols].rearrange("p (h j a) -> p h j a", a=1, j=SIDE)
                        last = nc.gpsimd.tensor_tensor(
                            kv[:, c, half * G2:(half + 1) * G2, :].rearrange("p h (j i) -> p h j i", i=SIDE),
                            cT.broadcast_to([P, G2, SIDE, SIDE]), vT.broadcast_to([P, G2, SIDE, SIDE]), ALU.mult)
                    last.then_inc(kv_ready.sem, 1)

            def skip_products(pool, row):
                sk_sum.wait(pool, row, back=1)
                nc.gpsimd.tensor_tensor(sk1[:], vcT[:, 0], vcT[:, 1], ALU.mult).then_inc(sk_mul.sem, 1)
                sk_mul.wait(pool, row, 1)
                nc.gpsimd.tensor_tensor(sk2[:], sk1[:],
                                        skip_sb[:].rearrange("p (a n) -> p a n", a=1).broadcast_to([P, KC, P]),
                                        ALU.mult).then_inc(sk_mul.sem, 1)

            def skip_out(pool, row):
                sk_sum.wait(pool, row)
                o2_ready.wait(pool, row, back=1)
                nc.gpsimd.tensor_tensor(skc[:].rearrange("p c (g j) -> p (c g) j", j=SIDE),
                                        vcT[:, 1].rearrange("p c (g j) -> p (c g) j", j=SIDE),
                                        sks[:].rearrange("p c (g a) -> p (c g) a", a=1)
                                        .broadcast_to([P, KC * GROUPS, SIDE]), ALU.mult).then_inc(sk_out.sem, 1)

            def conv_out(pool, row):
                gsum.wait(pool, row)
                sk_out.wait(pool, row)
                o2_T.wait(pool, row, back=1)
                nc.gpsimd.tensor_tensor(o2f[:], o2[:], skc[:], ALU.add).then_inc(o2_ready.sem, 1)

            def root(n):
                def piece(pool, row):
                    ln_step.wait(pool, row, 3 * n + 3)
                    nc.gpsimd.tensor_tensor(rstd[:], var[:], minus_half[:], ALU.pow).then_inc(rstd_ready.sem, 1)
                return piece

            nc.gpsimd.memset(minus_half[:], -0.5).then_inc(s_half, 1)
            pool.wait_ge(s_half, 1)
            pool.wait_ge(s_const, NCONST)
            pieces = {0: [root(0), add_bias], 3: [rope_sin(0), rope_sin(1), mask_keys],
                      5: [shift(0), shift(1)], 6: [shift(2), shift(3)], 12: [root(1)], 14: [products_kv, skip_products],
                      15: [skip_out], 18: [conv_out, root(2)]}
            steps(pool, pieces, none, none, none, none, none)


def rope_tables():
    pos = np.arange(P, dtype=np.float32)[:, None]
    exps = -np.arange(0, HD, 2, dtype=np.float32) / np.float32(HD)
    thetas = np.repeat(np.power(np.float32(10000.0), exps), 2)
    angles = (pos * thetas[None, :]).astype(np.float32)
    sign = np.where(np.arange(HD) % 2 == 0, -1.0, 1.0)
    cos = np.cos(angles).T
    sin = np.sin(angles).T * sign[:, None]
    return np.stack([np.tile(cos, (P // HD, 1)), np.tile(sin, (P // HD, 1))], axis=1).astype(np.float32)


def constants():
    at = np.arange(P)
    return {
        "trig": rope_tables(),
        "causal": np.where(at[None, :] > at[:, None], NEG, 0.0).astype(np.float32),
        "ident": np.eye(P, dtype=np.float32),
        "halves": np.stack([(at // HD) % 2 == 0, (at // HD) % 2 == 1], axis=1).astype(np.float32),
    }


def by_rows(w):
    return w.reshape(KC, P, -1).transpose(1, 0, 2)


def attention_weights(Wq, Wk, Wv, Wo, gate_w, gate_vec):
    swap = np.arange(E) ^ 1
    pad = np.zeros((E, AW - R0 - NR), np.float32)
    w = np.concatenate([Wq, Wq[:, swap], Wk, Wk[:, swap], Wv, Wo, gate_w.T, gate_vec.T, pad], axis=1)
    return by_rows(w).reshape(P, KC * AW)


def expert_weights(egu, ed, sgu, sd):
    gates = np.concatenate([egu[:, :INTER].reshape(-1, E), sgu[:SHARED]])
    ups = np.concatenate([egu[:, INTER:].reshape(-1, E), sgu[SHARED:]])
    downs = np.concatenate([ed.transpose(0, 2, 1).reshape(-1, E), sd.T])
    gu = np.stack([gates.reshape(NCHUNK, CHUNK, KC, P), ups.reshape(NCHUNK, CHUNK, KC, P)])
    gu = gu.transpose(1, 4, 3, 0, 2).reshape(NCHUNK, P, GU)
    dn = np.zeros((NCHUNK, DPAD, E), np.float32)
    dn[:, :CHUNK] = downs.reshape(NCHUNK, CHUNK, E)
    dn = dn.reshape(NCHUNK, DT, P, E).transpose(0, 2, 1, 3).reshape(NCHUNK, P, DT * E)
    return np.concatenate([gu, dn], axis=2)


def toeplitz(k):
    padded = np.concatenate([np.zeros((GROUPS, P - 1), np.float32), k], axis=1)
    at = P - 1 + np.arange(2 * P)[None, :] - np.arange(P)[:, None]
    return padded[:, at].transpose(1, 0, 2).reshape(P, GROUPS, 2, P)


def bias_columns(bq, bk):
    swap = np.arange(E) ^ 1
    return np.stack([b.reshape(KC, P)[c] for b in (bq, bq[swap], bk, bk[swap]) for c in range(KC)], axis=1)


def kernel(**inputs):
    import concourse.bacc as bacc
    from concourse.bass_utils import run_bass_kernel_spmd

    a = {n: np.asarray(v) for n, v in inputs.items()}
    arrays = {
        "x": a["x"], "ctx_in": a["ctx_2048"],
        "w_attn": attention_weights(a["L0_attn_Wq"], a["L0_attn_Wk"], a["L0_attn_Wv"], a["L0_attn_Wo"],
                                    a["L0_ffn_gate_w"], a["L0_ffn_shared_gate_vec"]),
        "w_moe": expert_weights(a["L0_ffn_expert_gate_up"], a["L0_ffn_expert_down"],
                                a["L0_ffn_shared_gate_up"], a["L0_ffn_shared_down"]),
        "toep": toeplitz(a["L0_xattn_k"]),
        "bias_qk": bias_columns(a["L0_attn_bq"], a["L0_attn_bk"]),
        "bias_v": a["L0_attn_bv"], "bias_o": a["L0_attn_bo"], "skip": a["fside_S2_0"],
        **constants(),
    }
    nc = bacc.Bacc("TRN2", target_bir_lowering=False, num_devices=1)
    args = {}
    arrays = {f"in_{n}": np.ascontiguousarray(v) for n, v in arrays.items()}
    for n, v in arrays.items():
        args[n[3:]] = nc.dram_tensor(n, v.shape, mybir.dt.from_np(v.dtype), kind="ExternalInput").ap()
    out = nc.dram_tensor("out_y", a["x"].shape, F32, kind="ExternalOutput").ap()
    build(nc, out=out, **args)
    r = run_bass_kernel_spmd(nc, [arrays], core_ids=[0])
    return r.results[0]["out_y"]
```

```python
from contextlib import ExitStack

import numpy as np
import concourse.bass as bass
from concourse import mybir

ALU = mybir.AluOpType
ACT = mybir.ActivationFunctionType
F32 = mybir.dt.float32
F16 = mybir.dt.float16
BF16 = mybir.dt.bfloat16
X = mybir.AxisListType.X

P = 128
E = 256
KC = E // P
HEADS, HD = 16, 16
GROUPS, SIDE = 16, 8
EXPERTS, TOP, INTER, SHARED = 16, 4, 176, 704
CHUNK = 512
INNER = SHARED + EXPERTS * INTER
NCHUNK = -(-INNER // CHUNK)
DT = CHUNK // P
UNIT = 2 * CHUNK
UNITS = KC + DT * E // UNIT
RING = 4
WS = 64.0
SILU = 0.5 / (WS * WS)
EPS = 1e-5
NEG = -1e30
QK, V0, O0, R0, NR = 8 * P, 8 * P, 8 * P + E, 8 * P + 2 * E, EXPERTS + 1
AW = R0 + 20


def width(c):
    return min(CHUNK, INNER - c * CHUNK)


def tiles(c):
    return [min(P, width(c) - t) for t in range(0, width(c), P)]


def segments(c):
    bounds = [(0, SHARED, EXPERTS)] + [(SHARED + e * INTER, SHARED + (e + 1) * INTER, e) for e in range(EXPERTS)]
    at, end = c * CHUNK, c * CHUNK + width(c)
    return [(max(lo, at) - at, min(hi, end) - at, e) for lo, hi, e in bounds if lo < end and hi > at]


class Row:

    def __init__(self, b, half, par):
        self.b, self.half, self.par = b, half, par


def numbered(b):
    return Row(b, b // 2, b % 2)


class Signal:

    def __init__(self, sem, per):
        self.sem, self.per = sem, per

    def value(self, row, k=None, back=0):
        k = self.per if k is None else k
        return row.b * self.per + (k - back * self.per)

    def wait(self, eng, row, k=None, back=0):
        if isinstance(row.b, int) and row.b < back:
            return
        eng.wait_ge(self.sem, self.value(row, k, back))


def build(nc, x, ctx_in, w_attn, w_moe, toep, bias_qk, bias_v, bias_o, skip,
          trig, causal, ident, halves, out):
    NB = x.shape[0]
    stack = ExitStack()
    with stack:
        def sb(name, shape, dt=F32):
            return stack.enter_context(nc.sbuf_tensor(name, shape, dt))

        def sem(name):
            return stack.enter_context(nc.semaphore(name))

        def signal(name, per=1):
            return Signal(sem(name), per)

        wa = [sb(f"w_attn_{n}", [P, KC, AW], F16) for n in ("hi", "lo")]
        wgu = [sb(f"w_gate_up_{n}", [P, NCHUNK, KC, 2, CHUNK], F16) for n in ("hi", "lo")]
        wd = [sb(f"w_down_{n}", [P, NCHUNK, DT, E], F16) for n in ("hi", "lo")]
        toep_w = [sb(f"toeplitz_{n}", [P, GROUPS, 2, P], F16) for n in ("hi", "lo")]
        bqk_sb = sb("bias_qk_sb", [P, 8])
        bv_sb = sb("bias_v_sb", [P, E])
        bo_sb = sb("bias_o_sb", [P, E])
        skip_sb = sb("skip_sb", [P, P])
        skip64 = sb("skip_scaled_once", [P, P])
        trig_sb = sb("trig_sb", [P, 2, 2, P])
        causal_sb = sb("causal_sb", [P, P])
        causal_b = sb("causal_bf16", [P, P], BF16)
        id_b = sb("identity_bf16", [P, P], BF16)
        id_sb = sb("identity", [P, P])
        halves_sb = sb("halves_sb", [P, 2])
        stage = sb("stage_moe", [P, RING, UNIT])
        x_sb = [sb(f"x_sb{i}", [P, E]) for i in range(2)]
        c_sb = [sb(f"ctx_sb{i}", [P, E]) for i in range(2)]
        xb = sb("x_plus_bias", [P, E])
        st6 = [sb(f"ln_stats{n}", [P, 6]) for n in range(3)]
        mv = [sb(f"ln_mean_var{n}", [P, 2]) for n in range(3)]
        var = [sb(f"ln_var{n}", [P, 1]) for n in range(3)]
        rstd = [sb(f"ln_rstd{n}", [P, 1]) for n in range(3)]
        xn = [sb(f"x_norm{n}", [P, E]) for n in range(3)]
        minus_half = sb("minus_half", [P, 1])
        tT = [sb(f"lhs_t_{n}", [P, KC, P], F16) for n in ("hi", "lo")]
        qkb = sb("qk_biased", [P, 8, P])
        qk = sb("qk_cos_then_roped", [P, 2, 2, P])
        rs = sb("rope_sin", [P, 2, 2, P])
        kmask = sb("k_by_parity", [P, 2, KC, P])
        v_f = sb("v_biased", [P, HEADS, HD])
        v_sb = [sb(f"v_{n}", [P, HEADS, HD + 1], F16) for n in ("hi", "lo")]
        sm = sb("probs", [P, 4, 4, P])
        pT = [sb(f"probs_t_{n}", [P, 4, 4, P], F16) for n in ("hi", "lo")]
        mx = sb("row_neg_max", [P, 4, 4])
        rsum = sb("softmax_recip", [P, HEADS])
        o_sb = sb("attn_out", [P, E])
        x1 = sb("x1", [P, E])
        vcT = sb("v_ctx_t", [P, 2, KC, P])
        scratch = sb("scratch", [P, 2 * GROUPS * P])
        stage_a = scratch[:, 0:KC * AW]
        kv = scratch[:, 0:2048].rearrange("p (c h n) -> p c h n", c=KC, h=GROUPS)
        z = scratch[:, 2048:3072]
        sk1, sk2, o2, o2f = (scratch[:, n:n + E].rearrange("p (c n) -> p c n", c=KC)
                             for n in range(3072, 4096, E))
        kvh = [sb(f"kv_{n}", [P, KC, GROUPS, SIDE * SIDE], F16) for n in ("hi", "lo")]
        sks = sb("skip_sum", [P, KC, GROUPS])
        skc = sb("skip_out", [P, KC, P])
        places = stage[:].rearrange("p r n -> p (r n)")
        late = iter(np.cumsum([0, E, E, CHUNK, CHUNK, CHUNK, CHUNK]).tolist())

        def take(n, dt=F32):
            at = next(late)
            return places[:, at:at + n] if dt == F32 else places[:, at:at + n].bitcast(dt)

        x2 = [sb("x2_0", [P, E]), take(E)]
        xT_odd = take(E, F16).rearrange("p (s c n) -> p s c n", s=2, c=KC)
        xT = [[sb(f"moe_x_t_{n}", [P, KC, P], F16) for n in ("hi", "lo")], [xT_odd[:, 0], xT_odd[:, 1]]]
        lg = sb("logits", [P, EXPERTS + 8 - TOP])
        top8 = sb("top8", [P, 8])
        picks = sb("picks", [P, 8])
        picked = sb("picked", [P, EXPERTS + 8 - TOP])
        lmax = sb("logit_neg_max", [P, 1])
        ex = sb("router_exp", [P, EXPERTS])
        gth = sb("gate_tanh", [P, 1])
        esel = sb("router_sel", [P, EXPERTS])
        esum = sb("router_sum", [P, 1])
        erec = sb("router_recip", [P, 1])
        cw = [sb(f"expert_weight{i}", [P, NR]) for i in range(2)]
        th = take(CHUNK)
        ga = take(CHUNK)
        hh = take(CHUNK)
        hT_both = take(CHUNK, F16).rearrange("p (s t n) -> p s t n", s=2, t=DT)
        hT = [hT_both[:, 0], hT_both[:, 1]]

        def bank(name):
            return stack.enter_context(nc.psum_tensor(name, [P, 512], F32))

        pg, pu, ph, pacc = bank("ps_gate"), bank("ps_up"), bank("ps_inner_t"), bank("ps_out")
        pf = stack.enter_context(nc.psum_tensor("ps_front", [P, 4, 512], F32))

        s_const = sem("const_loaded")
        s_wa = [sem(f"attn_weights_loaded{i}") for i in range(KC)]
        s_toep = sem("toeplitz_loaded")
        s_stage = [sem(f"moe_weights_loaded{i}") for i in range(RING)]
        s_x = [sem(f"x_loaded{i}") for i in range(2)]
        s_c = [sem(f"ctx_loaded{i}") for i in range(2)]
        s_y = [sem(f"y_stored{i}") for i in range(2)]
        s_wa_hi, s_wa_lo = sem("attn_hi_done"), sem("attn_lo_done")
        s_t_hi, s_t_lo = sem("toeplitz_hi_done"), sem("toeplitz_lo_done")
        s_w_hi, s_w_lo = sem("moe_hi_done"), sem("moe_lo_done")
        s_once = sem("constants_set")
        s_half = sem("minus_half_set")
        s_tables = sem("tables_loaded")

        ln_step = [signal(f"ln{n}_step", 3) for n in range(3)]
        rstd_ready = [signal(f"ln{n}_rstd") for n in range(3)]
        normed = [signal(f"ln{n}_done") for n in range(3)]
        xb_ready = signal("x_plus_bias_ready")
        xn_T = signal("xn_transposed")
        lhs_hi = signal("lhs_hi", 2)
        lhs_lo = signal("lhs_lo", 2)
        q_ready = signal("q_projected")
        k_ready = signal("k_projected")
        v_ready = signal("v_projected")
        qk_biased = signal("qk_biased", 2)
        v_done = signal("v_done")
        v_hi = signal("v_hi")
        v_lo = signal("v_lo")
        cos_done = signal("cos_done", 2)
        sin_done = signal("sin_done", 2)
        roped = signal("roped", 2)
        k_masked = signal("k_masked")
        scored = signal("scored", 2)
        maxed = signal("maxed", 4)
        exped = signal("exped", 4)
        probs_T = signal("probs_transposed", 4)
        pT_hi = signal("probs_t_hi", 4)
        pT_lo = signal("probs_t_lo", 4)
        av_ready = signal("av_ready")
        recip_done = signal("recip_done")
        o_ready = signal("attn_out_ready")
        o_T = signal("attn_out_transposed")
        wo_ready = signal("wo_ready")
        x1_ready = signal("x1_ready")
        vc_T = signal("v_ctx_transposed")
        vc_ready = signal("v_ctx_ready")
        kv_ready = signal("kv_ready", 2)
        kv_hi = signal("kv_hi", 2)
        kv_lo = signal("kv_lo", 2)
        sk_mul = signal("skip_multiplied", 2)
        sk_sum = signal("skip_summed")
        sk_out = signal("skip_out_done")
        conv_ready = signal("conv_ready", 2)
        gated = signal("conv_gated", 4)
        gsum = signal("conv_summed", 4)
        o2_ready = signal("conv_out_ready")
        o2_T = signal("conv_out_transposed")
        x2_ready = signal("x2_ready")
        xn3_T = signal("xn3_transposed")
        xT_hi = signal("moe_x_hi")
        xT_lo = signal("moe_x_lo")
        routed = signal("router_logits")
        lg_ready = signal("logits_ready")
        lmax_ready = signal("logit_max_ready")
        gth_ready = signal("shared_gate_tanh_ready")
        ex_ready = signal("router_exp_ready")
        top_ready = signal("top8_ready")
        pick_done = signal("pick_done", 2)
        sel_done = signal("select_done", 3)
        cw_ready = signal("expert_weight_ready", 2)

        NC = NCHUNK
        gate_ready = signal("gate_ready", NC)
        up_ready = signal("up_ready", NC)
        tanh_done = signal("tanh_done", NC)
        gate_done = signal("gate_done", NC)
        inner_done = signal("inner_done", NC)
        inner_T = signal("inner_transposed", NC)
        inner_hi = signal("inner_hi", NC)
        inner_lo = signal("inner_lo", NC)
        down_done = signal("down_done", NC)
        y_ready = signal("y_ready")

        ring = lambda g: pf[:, g, :]

        def products(first, last):
            terms = ((0, 0), (0, 1), (1, 0))
            return [(a, b, first and n == 0, last and n == 2) for n, (a, b) in enumerate(terms)]

        ATT, MIX, MOE = 0, 1, 2

        def step(eng, att, mix, moe, prev, pieces, gate, turn, up, down, finish, fill=None):
            rows = (att, mix, moe)

            def run(at):
                for which, piece in pieces.get(at, ()):
                    if rows[which] is not None:
                        piece(eng, rows[which])

            for c in range(NC):
                before = (moe, c - 1) if c > 0 else (prev, NC - 1)
                if before[0] is not None:
                    turn(eng, *before)
                run(c)
                if moe is not None:
                    gate(eng, moe, c)
                    up(eng, moe, c)
                if fill is not None:
                    fill(c)
                run(c + .3)
                if before[0] is not None:
                    down(eng, *before)
                    if c == 0:
                        finish(eng, prev)
                run(c + .6)

        FIRST = [0, 0, 2, 3, 1, 2, 2]
        SECOND = [1, 1, 2, 3, 2, 2, 0]

        def steps(eng, *fns, prepare=None):
            def fill(start, units):
                def run(c):
                    for u in range(sum(units[:c]), sum(units[:c + 1])):
                        prepare(eng, start + u)
                return prepare and run

            step(eng, numbered(0), None, None, None, *fns, fill=fill(0, FIRST))
            step(eng, numbered(1), numbered(0), None, None, *fns, fill=fill(sum(FIRST), SECOND))
            step(eng, numbered(2), numbered(1), numbered(0), None, *fns)
            step(eng, numbered(3), numbered(2), numbered(1), numbered(0), *fns)
            with eng.Fori(0, (NB - 4) // 2) as i:
                step(eng, Row(2 * i + 4, i + 2, 0), Row(2 * i + 3, i + 1, 1), Row(2 * i + 2, i + 1, 0),
                     Row(2 * i + 1, i, 1), *fns)
                step(eng, Row(2 * i + 5, i + 2, 1), Row(2 * i + 4, i + 2, 0), Row(2 * i + 3, i + 1, 1),
                     Row(2 * i + 2, i + 1, 0), *fns)
            step(eng, None, numbered(NB - 1), numbered(NB - 2), numbered(NB - 3), *fns)
            step(eng, None, None, numbered(NB - 1), numbered(NB - 2), *fns)
            turn, down, finish = fns[2], fns[4], fns[5]
            turn(eng, numbered(NB - 1), NC - 1)
            down(eng, numbered(NB - 1), NC - 1)
            finish(eng, numbered(NB - 1))

        NCONST = 16 * 8
        TOEP_AT = 5

        def unit_of(half, c, n):
            if n < KC:
                return wgu[half][:, c, n].rearrange("p s n -> p (s n)")
            return wd[half][:, c].rearrange("p t n -> p (t n)")

        def wait_apart(eng, *waits):
            values = [v if isinstance(v, int) else eng.to_reg(v) for _, v in waits]
            eng.wait_ge(s_const, NCONST)
            for (semaphore, _), value in zip(waits, values):
                eng.wait_ge(semaphore, value)

        none = lambda *a: None
        block = stack.enter_context(nc.Block())

        @block.sync
        def _(sp):
            def load_x(row):
                if not (isinstance(row.b, int) and row.b < 2):
                    wait_apart(sp, (normed[0].sem, normed[0].value(row, back=2)),
                               (xb_ready.sem, xb_ready.value(row, back=2)))
                sp.dma_start(x_sb[row.par][:], x[row.b]).then_inc(s_x[row.par], 16)

            def load_ctx(row):
                if not (isinstance(row.b, int) and row.b < 2):
                    wait_apart(sp, (vc_T.sem, vc_T.value(row, back=2)))
                sp.dma_start(c_sb[row.par][:], ctx_in[row.b]).then_inc(s_c[row.par], 16)

            def store_row(row):
                wait_apart(sp, (y_ready.sem, y_ready.value(row)))
                sp.dma_start(out[row.b], x2[row.par][:]).then_inc(s_y[row.par], 16)

            for dst, src in ((id_sb, ident), (bqk_sb, bias_qk), (trig_sb, trig), (causal_sb, causal),
                             (halves_sb, halves)):
                sp.dma_start(dst[:], src).then_inc(s_const, 16)
            for dst, src in ((bv_sb, bias_v), (bo_sb, bias_o), (skip_sb, skip)):
                sp.dma_start(dst[:], src.partition_broadcast(P)).then_inc(s_const, 16)
            sp.dma_start(stage_a[:, 0:AW], w_attn[:, 0:AW]).then_inc(s_wa[0], 16)
            load_x(numbered(0))
            sp.dma_start(stage_a[:, AW:KC * AW], w_attn[:, AW:KC * AW]).then_inc(s_wa[1], 16)
            load_x(numbered(1))
            for r in range(2):
                load_ctx(numbered(r))
            for u in range(NC * UNITS):
                if u == RING:
                    sp.wait_ge(s_wa_lo, KC)
                    sp.dma_start(scratch[:], toep).then_inc(s_toep, 16)
                if u >= RING:
                    sp.wait_ge(s_w_lo, u - RING + 1)
                sp.dma_start(stage[:, u % RING], w_moe[u]).then_inc(s_stage[u % RING], 16)
            load_x(numbered(2))
            load_x(numbered(3))
            load_ctx(numbered(2))
            for r in range(2):
                store_row(numbered(r))
                load_x(numbered(r + 4))
                load_ctx(numbered(r + 3))
            with sp.Fori(0, (NB - 6) // 2) as i:
                store_row(Row(2 * i + 2, i + 1, 0))
                load_x(Row(2 * i + 6, i + 3, 0))
                load_ctx(Row(2 * i + 5, i + 2, 1))
                store_row(Row(2 * i + 3, i + 1, 1))
                load_x(Row(2 * i + 7, i + 3, 1))
                load_ctx(Row(2 * i + 6, i + 3, 0))
            store_row(numbered(NB - 4))
            load_ctx(numbered(NB - 1))
            for r in range(NB - 3, NB):
                store_row(numbered(r))
            for par in range(2):
                sp.wait_ge(s_y[par], 16 * (NB // 2))

        @block.tensor
        def _(pe):
            def t_norm(pe, row):
                normed[0].wait(pe, row)
                lhs_lo.wait(pe, row, back=1)
                for c in range(KC):
                    last = nc.tensor.transpose(ring(3)[:, c * P:(c + 1) * P], xn[0][:, c * P:(c + 1) * P], id_sb[:])
                last.then_inc(xn_T.sem, 1)

            def project_qk(pe, row):
                lhs_hi.wait(pe, row, 1)
                lhs_lo.wait(pe, row, 1)
                x1_ready.wait(pe, row, back=1)
                for side, ready in ((0, q_ready), (1, k_ready)):
                    for t in range(4):
                        col = (4 * side + t) * P
                        for kc in range(KC):
                            for a, b, first, end in products(kc == 0, kc == KC - 1):
                                last = nc.tensor.matmul(ring(2 + side)[:, t * P:(t + 1) * P],
                                                        wa[a][:, kc, col:col + P], tT[b][:, kc, :],
                                                        start=first, stop=end)
                    last.then_inc(ready.sem, 1)

            def project_v(pe, row):
                qk_biased.wait(pe, row, 1)
                for kc in range(KC):
                    for a, b, first, end in products(kc == 0, kc == KC - 1):
                        last = nc.tensor.matmul(ring(2)[:, 0:E], tT[a][:, kc, :], wa[b][:, kc, V0:V0 + E],
                                                start=first, stop=end)
                last.then_inc(v_ready.sem, 1)

            def scores(half):
                def piece(pe, row):
                    if half == 0:
                        roped.wait(pe, row)
                        k_masked.wait(pe, row)
                        qk_biased.wait(pe, row)
                        v_done.wait(pe, row)
                    else:
                        exped.wait(pe, row, 2)
                    for bank in (2, 3):
                        nc.tensor.matmul(ring(bank).rearrange("p (s n) -> p s n", n=P), id_b[:], causal_b[:].rearrange("p (a n) -> p a n", a=1).broadcast_to([P, 4, P]),
                                         start=True, stop=False, skip_group_check=True)
                    for c in range(KC):
                        for e in range(2):
                            for g in range(2 * half, 2 * half + 2):
                                rows = slice(32 * g, 32 * g + 32)
                                s = 2 * c + e
                                last = nc.tensor.matmul(ring(2 + g % 2)[:, s * P:(s + 1) * P], qk[rows, 0, c, :],
                                                        kmask[rows, e, c, :], start=False, stop=True,
                                                        skip_group_check=True)
                    last.then_inc(scored.sem, 1)
                return piece

            def t_probs(g):
                def piece(pe, row):
                    exped.wait(pe, row, g + 1)
                    if g < 2:
                        exped.wait(pe, row, g + 3)
                    else:
                        pT_lo.wait(pe, row, g - 1)
                    for s in range(4):
                        last = nc.tensor.transpose(ring(2 + g % 2)[:, s * P:(s + 1) * P], sm[:, g, s, :], id_sb[:])
                    last.then_inc(probs_T.sem, 1)
                return piece

            def attend(pe, row):
                pT_hi.wait(pe, row)
                pT_lo.wait(pe, row)
                v_hi.wait(pe, row)
                v_lo.wait(pe, row)
                for h in range(HEADS):
                    g, s = (h % 8) // 2, 2 * (h // 8) + h % 2
                    for a, b, first, end in products(True, True):
                        last = nc.tensor.matmul(ring(2)[:, h * 17:h * 17 + 17], pT[a][:, g, s, :],
                                                v_sb[b][:, h, :], start=first, stop=end)
                last.then_inc(av_ready.sem, 1)

            def t_attn(pe, row):
                o_ready.wait(pe, row)
                for c in range(KC):
                    last = nc.tensor.transpose(ring(3)[:, c * P:(c + 1) * P], o_sb[:, c * P:(c + 1) * P], id_sb[:])
                last.then_inc(o_T.sem, 1)

            def out_proj(pe, row):
                lhs_hi.wait(pe, row, 2)
                lhs_lo.wait(pe, row, 2)
                for kc in range(KC):
                    for a, b, first, end in products(kc == 0, kc == KC - 1):
                        last = nc.tensor.matmul(ring(2)[:, 0:E], tT[a][:, kc, :], wa[b][:, kc, O0:O0 + E],
                                                start=first, stop=end)
                last.then_inc(wo_ready.sem, 1)

            def t_vc(pe, row):
                normed[1].wait(pe, row)
                pe.wait_ge(s_c[row.par], row.half * 16 + 16)
                lg_ready.wait(pe, row, back=1)
                gth_ready.wait(pe, row, back=1)
                for n, src in ((0, xn[1]), (1, c_sb[row.par])):
                    for c in range(KC):
                        at = (2 * n + c) * P
                        last = nc.tensor.transpose(ring(0)[:, at:at + P], src[:, c * P:(c + 1) * P], id_sb[:])
                last.then_inc(vc_T.sem, 1)

            def conv(half):
                def piece(pe, row):
                    kv_hi.wait(pe, row, half + 1)
                    kv_lo.wait(pe, row, half + 1)
                    if half == 0:
                        vc_ready.wait(pe, row)
                        xT_lo.wait(pe, row, back=1)
                        if isinstance(row.b, int) and row.b == 0:
                            pe.wait_ge(s_t_hi, 1)
                            pe.wait_ge(s_t_lo, 1)
                    else:
                        gated.wait(pe, row, 2)
                    for h in range(8 * half, 8 * half + 8):
                        to = ring(h // 4 % 2)[:, (h % 4) * P:(h % 4) * P + P]
                        for a, b, first, end in products(True, False):
                            nc.tensor.matmul(to.rearrange("p (c n) -> p c n", c=2), toep_w[a][:, h, 0, :],
                                             kvh[b][:, :, h, :], start=first, stop=end, skip_group_check=True)
                        for a, b, first, end in products(False, True):
                            last = nc.tensor.matmul(to[:, 64:128], toep_w[a][:, h, 1, :], kvh[b][:, 0, h, :],
                                                    start=first, stop=end, skip_group_check=True)
                    last.then_inc(conv_ready.sem, 1)
                return piece

            def t_conv(pe, row):
                o2_ready.wait(pe, row)
                gated.wait(pe, row)
                for c in range(KC):
                    last = nc.tensor.transpose(ring(0)[:, c * P:(c + 1) * P], o2f[:, c, :], id_sb[:])
                last.then_inc(o2_T.sem, 1)

            def t_norm3(pe, row):
                normed[2].wait(pe, row)
                for c in range(KC):
                    last = nc.tensor.transpose(ring(1)[:, c * P:(c + 1) * P], xn[2][:, c * P:(c + 1) * P], id_sb[:])
                last.then_inc(xn3_T.sem, 1)

            def router(pe, row):
                xT_hi.wait(pe, row)
                xT_lo.wait(pe, row)
                x2_ready.wait(pe, row)
                n = 0
                for kc in range(KC):
                    for a in range(2):
                        for b in range(2):
                            last = nc.tensor.matmul(ring(0)[:, 0:NR], xT[row.par][a][:, kc, :],
                                                    wa[b][:, kc, R0:R0 + NR], start=n == 0, stop=n == 7)
                            n += 1
                last.then_inc(routed.sem, 1)

            def half_product(bank, side, pe, row, c, ready):
                for kc in range(KC):
                    for a, b, first, end in products(kc == 0, kc == KC - 1):
                        last = nc.tensor.matmul(bank[:, 0:width(c)], xT[row.par][a][:, kc, :],
                                                wgu[b][:, c, kc, side, 0:width(c)], start=first, stop=end)
                last.then_inc(ready.sem, 1)

            def gate(pe, row, c):
                if c == 0:
                    xT_hi.wait(pe, row)
                    xT_lo.wait(pe, row)
                    gate_done.wait(pe, row, back=1)
                else:
                    gate_done.wait(pe, row, c)
                if isinstance(row.b, int) and row.b == 0 and c == 0:
                    pe.wait_ge(s_w_lo, NC * UNITS)
                    pe.wait_ge(s_w_hi, NC * UNITS)
                half_product(pg, 0, pe, row, c, gate_ready)

            def up(pe, row, c):
                if c == 0:
                    inner_done.wait(pe, row, back=1)
                else:
                    inner_done.wait(pe, row, c)
                half_product(pu, 1, pe, row, c, up_ready)

            def turn(pe, row, c):
                inner_done.wait(pe, row, c + 1)
                if c == 0:
                    inner_lo.wait(pe, row, back=1)
                else:
                    inner_lo.wait(pe, row, c)
                for t, n in enumerate(tiles(c)):
                    last = nc.tensor.transpose(ph[0:n, t * P:(t + 1) * P], hh[:, t * P:t * P + n], id_sb[:])
                last.then_inc(inner_T.sem, 1)

            def down(pe, row, c):
                inner_hi.wait(pe, row, c + 1)
                inner_lo.wait(pe, row, c + 1)
                if c == 0:
                    y_ready.wait(pe, row, back=1)
                for t, n in enumerate(tiles(c)):
                    for a, b, first, end in products(c == 0 and t == 0, c == NC - 1 and t == len(tiles(c)) - 1):
                        last = nc.tensor.matmul(pacc[:, 0:E], hT[a][0:n, t, :], wd[b][0:n, c, t, :],
                                                start=first, stop=end)
                last.then_inc(down_done.sem, 1)

            pe.wait_ge(s_const, NCONST)
            pe.wait_ge(s_wa_lo, KC)
            pe.wait_ge(s_once, 7)
            pieces = {0.3: [(MIX, attend)], 0.6: [(MIX, t_attn)], 1.3: [(MIX, out_proj), (ATT, t_norm)],
                      2.3: [(MIX, t_vc), (ATT, project_qk)], 2.6: [(ATT, project_v)],
                      3.3: [(ATT, scores(0))], 3.6: [(MIX, conv(0))],
                      4.3: [(ATT, scores(1))], 4.6: [(MIX, conv(1))],
                      5.3: [(ATT, t_probs(0)), (ATT, t_probs(1))], 5.6: [(MIX, t_conv)],
                      6.3: [(ATT, t_probs(2)), (MIX, t_norm3), (ATT, t_probs(3))], 6.6: [(MIX, router)]}
            steps(pe, pieces, gate, turn, up, down, none)

        @block.scalar
        def _(act):
            def lhs_split(n):
                def piece(act, row):
                    (xn_T, o_T)[n].wait(act, row)
                    if n == 0:
                        wo_ready.wait(act, row, back=1)
                    else:
                        v_ready.wait(act, row)
                    nc.scalar.activation(tT[0][:].rearrange("p c n -> p (c n)"), ring(3)[:, 0:E],
                                         ACT.Copy).then_inc(lhs_hi.sem, 1)
                return piece

            def biased(side):
                def piece(act, row):
                    (q_ready, k_ready)[side].wait(act, row)
                    cos_done.wait(act, row, back=1)
                    sin_done.wait(act, row, back=1)
                    for t in range(4):
                        n = 4 * side + t
                        last = nc.scalar.activation(qkb[:, n, :], ring(2 + side)[:, t * P:(t + 1) * P],
                                                    ACT.Identity, bias=bqk_sb[:, n:n + 1], scale=1.0 / WS)
                    last.then_inc(qk_biased.sem, 1)
                return piece

            def split_v(act, row):
                v_done.wait(act, row)
                av_ready.wait(act, row, back=1)
                nc.scalar.activation(v_sb[0][:, :, 0:HD], v_f[:], ACT.Copy).then_inc(v_hi.sem, 1)

            def exp_probs(g):
                def piece(act, row):
                    maxed.wait(act, row, g + 1)
                    probs_T.wait(act, row, g + 1, back=1)
                    for s in range(4):
                        last = nc.scalar.activation(sm[:, g, s, :], ring(2 + g % 2)[:, s * P:(s + 1) * P],
                                                    ACT.Exp, bias=mx[:, g, s:s + 1])
                    last.then_inc(exped.sem, 1)
                return piece

            def copy_probs(g):
                def piece(act, row):
                    probs_T.wait(act, row, g + 1)
                    av_ready.wait(act, row, back=1)
                    nc.scalar.activation(pT[0][:, g, :, :].rearrange("p s n -> p (s n)"), ring(2 + g % 2),
                                         ACT.Copy).then_inc(pT_hi.sem, 1)
                return piece

            def split_kv(half):
                def piece(act, row):
                    kv_ready.wait(act, row, half + 1)
                    conv_ready.wait(act, row, half + 1, back=1)
                    groups = slice(8 * half, 8 * half + 8)
                    nc.scalar.activation(kvh[0][:, :, groups, :], kv[:, :, groups, :], ACT.Copy)\
                        .then_inc(kv_hi.sem, 1)
                return piece

            def copy_vc(act, row):
                vc_T.wait(act, row)
                gated.wait(act, row, back=1)
                o2_ready.wait(act, row, back=1)
                kv_ready.wait(act, row, back=1)
                nc.scalar.activation(vcT[:].rearrange("p a c n -> p (a c n)"), ring(0),
                                     ACT.Copy).then_inc(vc_ready.sem, 1)

            def moe_x_hi(act, row):
                xn3_T.wait(act, row)
                if not (isinstance(row.b, int) and row.b < 2):
                    up_ready.wait(act, row, back=2)
                nc.scalar.activation(xT[row.par][0][:].rearrange("p c n -> p (c n)"), ring(1)[:, 0:E],
                                     ACT.Copy).then_inc(xT_hi.sem, 1)

            def gate_tanh(act, row):
                routed.wait(act, row)
                cw_ready.wait(act, row, 1, back=1)
                nc.scalar.activation(gth[:], ring(0)[:, EXPERTS:NR], ACT.Tanh, scale=0.5 / WS)\
                    .then_inc(gth_ready.sem, 1)

            def router_exp(act, row):
                lmax_ready.wait(act, row)
                sel_done.wait(act, row, back=1)
                nc.scalar.activation(ex[:], lg[:, 0:EXPERTS], ACT.Exp, bias=lmax[:]).then_inc(ex_ready.sem, 1)

            def gate(act, row, c):
                gate_ready.wait(act, row, c + 1)
                if isinstance(row.b, int) and row.b == 0 and c == 0:
                    act.wait_ge(s_w_lo, NC * UNITS)
                if c == 0:
                    gate_done.wait(act, row, back=1)
                else:
                    gate_done.wait(act, row, c)
                nc.scalar.activation(th[:, 0:width(c)], pg[:, 0:width(c)], ACT.Tanh, scale=0.5 / WS).then_inc(tanh_done.sem, 1)

            def turn(act, row, c):
                inner_T.wait(act, row, c + 1)
                if c == 0:
                    down_done.wait(act, row, back=1)
                else:
                    down_done.wait(act, row, c)
                nc.scalar.activation(hT[0][:].rearrange("p t n -> p (t n)"), ph[:, 0:CHUNK],
                                     ACT.Copy).then_inc(inner_hi.sem, 1)

            act.wait_ge(s_const, NCONST)
            act.wait_ge(s_half, 1)
            nc.scalar.activation(gth[:], minus_half[:], ACT.Tanh).then_inc(s_tables, 1)
            for kc in range(KC):
                act.wait_ge(s_wa[kc], 16)
                nc.scalar.activation(wa[0][:, kc, :], stage_a[:, kc * AW:(kc + 1) * AW], ACT.Copy,
                                     scale=WS).then_inc(s_wa_hi, 1)

            def split_toeplitz(act):
                act.wait_ge(s_toep, 16)
                nc.scalar.activation(toep_w[0][:].rearrange("p g c n -> p (g c n)"), scratch[:], ACT.Copy,
                                     scale=WS).then_inc(s_t_hi, 1)

            def prepare(act, u):
                if u == TOEP_AT:
                    split_toeplitz(act)
                c, n = divmod(u, UNITS)
                act.wait_ge(s_stage[u % RING], 16 * (u // RING + 1))
                nc.scalar.activation(unit_of(0, c, n), stage[:, u % RING], ACT.Copy, scale=WS)\
                    .then_inc(s_w_hi, 1)

            pieces = {0: [(MOE, router_exp)], 0.6: [(MIX, lhs_split(1))], 1.3: [(ATT, lhs_split(0))],
                      2.3: [(MIX, copy_vc), (ATT, biased(0)), (ATT, biased(1)), (MIX, split_kv(0))],
                      3.3: [(ATT, split_v), (MIX, split_kv(1)), (ATT, exp_probs(0)), (ATT, exp_probs(1))],
                      4.3: [(ATT, exp_probs(2)), (ATT, exp_probs(3))],
                      5.3: [(ATT, copy_probs(0)), (ATT, copy_probs(1))],
                      6.3: [(ATT, copy_probs(2)), (MIX, moe_x_hi), (ATT, copy_probs(3))],
                      6.6: [(MIX, gate_tanh)]}
            steps(act, pieces, gate, turn, none, none, none, prepare=prepare)

        @block.vector
        def _(dve):
            def norm(n, src_of, ready, used):
                def stats(dve, row):
                    ready(dve, row)
                    nc.vector.bn_stats(st6[n][:], src_of(row)).then_inc(ln_step[n].sem, 1)
                    wait_apart(dve, (ln_step[n].sem, ln_step[n].value(row, 1)))
                    nc.vector.bn_aggr(mv[n][:], st6[n][:]).then_inc(ln_step[n].sem, 1)
                    ln_step[n].wait(dve, row, 2)
                    nc.vector.tensor_scalar(var[n][:], mv[n][:, 1:2], EPS, None, ALU.add)\
                        .then_inc(ln_step[n].sem, 1)

                def result(dve, row):
                    rstd_ready[n].wait(dve, row)
                    used.wait(dve, row, back=1)
                    nc.vector.tensor_scalar(xn[n][:], src_of(row), mv[n][:, 0:1], rstd[n][:],
                                            ALU.subtract, ALU.mult).then_inc(normed[n].sem, 1)
                return stats, result

            norm1 = norm(0, lambda row: x_sb[row.par][:],
                         lambda dve, row: dve.wait_ge(s_x[row.par], row.half * 16 + 16), xn_T)
            norm2 = norm(1, lambda row: x1[:], lambda dve, row: x1_ready.wait(dve, row), vc_T)
            norm3 = norm(2, lambda row: x2[row.par][:], lambda dve, row: x2_ready.wait(dve, row), xn3_T)

            def lhs_split(n):
                def piece(dve, row):
                    lhs_hi.wait(dve, row, n + 1)
                    nc.vector.tensor_tensor(tT[1][:].rearrange("p c n -> p (c n)"), ring(3)[:, 0:E],
                                            tT[0][:].rearrange("p c n -> p (c n)"), ALU.subtract)\
                        .then_inc(lhs_lo.sem, 1)
                return piece

            def v_bias(dve, row):
                v_ready.wait(dve, row)
                nc.vector.scalar_tensor_tensor(
                    out=v_f[:], in0=ring(2)[:, 0:E].rearrange("p (h d) -> p h d", d=HD), scalar=1.0 / WS,
                    in1=bv_sb[:].rearrange("p (h d) -> p h d", d=HD), op0=ALU.mult, op1=ALU.add)\
                    .then_inc(v_done.sem, 1)

            def split_v(dve, row):
                v_hi.wait(dve, row)
                nc.vector.tensor_tensor(v_sb[1][:, :, 0:HD], v_f[:], v_sb[0][:, :, 0:HD], ALU.subtract)\
                    .then_inc(v_lo.sem, 1)

            def split_probs(g):
                def piece(dve, row):
                    pT_hi.wait(dve, row, g + 1)
                    nc.vector.tensor_tensor(pT[1][:, g, :, :].rearrange("p s n -> p (s n)"), ring(2 + g % 2),
                                            pT[0][:, g, :, :].rearrange("p s n -> p (s n)"), ALU.subtract)\
                        .then_inc(pT_lo.sem, 1)
                return piece

            def rope(side):
                def piece(dve, row):
                    qk_biased.wait(dve, row, side + 1)
                    scored.wait(dve, row, back=1)
                    cos = trig_sb[:, side, 0:1, :].broadcast_to([P, 2, P])
                    nc.vector.tensor_tensor(qk[:, side], qkb[:, 4 * side:4 * side + 2, :], cos, ALU.mult)\
                        .then_inc(cos_done.sem, 1)
                    cos_done.wait(dve, row, side + 1)
                    sin_done.wait(dve, row, side + 1)
                    nc.vector.tensor_tensor(qk[:, side], qk[:, side], rs[:, side], ALU.add).then_inc(roped.sem, 1)
                return piece

            def mask_keys(dve, row):
                roped.wait(dve, row)
                scored.wait(dve, row, back=1)
                for e in range(2):
                    last = nc.vector.tensor_scalar(kmask[:, e], qk[:, 1], halves_sb[:, e:e + 1], None, ALU.mult)
                last.then_inc(k_masked.sem, 1)

            def row_max(g):
                def piece(dve, row):
                    scored.wait(dve, row, g // 2 + 1)
                    nc.vector.tensor_reduce(mx[:, g, :], ring(2 + g % 2).rearrange("p (s n) -> p s n", n=P), X,
                                            ALU.max, negate=True).then_inc(maxed.sem, 1)
                return piece

            def normalise(dve, row):
                av_ready.wait(dve, row)
                o = ring(2)[:, 0:HEADS * 17].rearrange("p (h d) -> p h d", d=17)
                nc.vector.reciprocal(rsum[:].rearrange("p (h a) -> p h a", a=1), o[:, :, HD:HD + 1])\
                    .then_inc(recip_done.sem, 1)
                recip_done.wait(dve, row)
                o_T.wait(dve, row, back=1)
                nc.vector.tensor_tensor(o_sb[:].rearrange("p (h d) -> p h d", d=HD), o[:, :, 0:HD],
                                        rsum[:].rearrange("p (h a) -> p h a", a=1).broadcast_to([P, HEADS, HD]),
                                        ALU.mult).then_inc(o_ready.sem, 1)

            def residual1(dve, row):
                wo_ready.wait(dve, row)
                xb_ready.wait(dve, row)
                x2_ready.wait(dve, row, back=1)
                nc.vector.scalar_tensor_tensor(out=x1[:], in0=ring(2)[:, 0:E], scalar=1.0 / WS, in1=xb[:],
                                               op0=ALU.mult, op1=ALU.add).then_inc(x1_ready.sem, 1)

            def skip_sum(dve, row):
                sk_mul.wait(dve, row)
                sk_out.wait(dve, row, back=1)
                nc.vector.tensor_reduce(sks[:].rearrange("p c g -> p (c g)"),
                                        sk2[:].rearrange("p c (g i) -> p (c g) i", i=SIDE),
                                        X, ALU.add).then_inc(sk_sum.sem, 1)

            def gate_conv(half, c):
                def piece(dve, row):
                    k = 2 * half + c
                    conv_ready.wait(dve, row, half + 1)
                    if k > 0:
                        gsum.wait(dve, row, k)
                    else:
                        gsum.wait(dve, row, back=1)
                        o2_ready.wait(dve, row, back=1)
                    G2 = GROUPS // 2
                    y = pf[:, 0:2, :].rearrange("p b (h c n) -> p (b h) c n", h=4, c=2)[:, :, c, :]
                    y = y.rearrange("p h (j i) -> p h j i", i=SIDE)
                    cT = vcT[:, 1, c, half * 64:half * 64 + 64].rearrange("p (h a i) -> p h a i", a=1, i=SIDE)
                    zz = z[:, k % 2 * 512:k % 2 * 512 + 512].rearrange("p (h j i) -> p h j i", j=SIDE, i=SIDE)
                    nc.vector.tensor_tensor(zz, y, cT.broadcast_to([P, G2, SIDE, SIDE]), ALU.mult)\
                        .then_inc(gated.sem, 1)
                    gated.wait(dve, row, k + 1)
                    nc.vector.tensor_reduce(o2[:, c, half * 64:half * 64 + 64],
                                            z[:, k % 2 * 512:k % 2 * 512 + 512].rearrange("p (n i) -> p n i", i=SIDE),
                                            X, ALU.add).then_inc(gsum.sem, 1)
                return piece

            def residual2(dve, row):
                o2_T.wait(dve, row)
                if not (isinstance(row.b, int) and row.b < 2):
                    dve.wait_ge(s_y[row.par], row.half * 16)
                nc.vector.scalar_tensor_tensor(out=x2[row.par][:], in0=ring(0)[:, 0:E], scalar=1.0 / WS, in1=x1[:],
                                               op0=ALU.mult, op1=ALU.add).then_inc(x2_ready.sem, 1)

            def moe_x_lo(dve, row):
                xT_hi.wait(dve, row)
                nc.vector.tensor_tensor(xT[row.par][1][:].rearrange("p c n -> p (c n)"), ring(1)[:, 0:E],
                                        xT[row.par][0][:].rearrange("p c n -> p (c n)"), ALU.subtract)\
                    .then_inc(xT_lo.sem, 1)

            def logits(dve, row):
                gth_ready.wait(dve, row)
                ex_ready.wait(dve, row, back=1)
                nc.vector.tensor_scalar(lg[:, 0:EXPERTS], ring(0)[:, 0:EXPERTS], 1.0 / WS, None, ALU.mult)\
                    .then_inc(lg_ready.sem, 1)
                inner_done.wait(dve, row, back=2)
                nc.vector.tensor_scalar(cw[row.par][:, EXPERTS:NR], gth[:], 1.0, 0.5 * SILU, ALU.add, ALU.mult)\
                    .then_inc(cw_ready.sem, 1)

            def top(dve, row):
                wait_apart(dve, (lg_ready.sem, lg_ready.value(row)))
                nc.vector.max(top8[:], lg[:, 0:EXPERTS]).then_inc(top_ready.sem, 1)
                top_ready.wait(dve, row)
                nc.vector.tensor_scalar(lmax[:], top8[:, 0:1], -1.0, None, ALU.mult).then_inc(lmax_ready.sem, 1)

            def choose(dve, row):
                nc.vector.tensor_copy(picks[:, 0:TOP], top8[:, 0:TOP]).then_inc(pick_done.sem, 1)
                wait_apart(dve, (pick_done.sem, pick_done.value(row, 1)))
                nc.vector.match_replace(out=picked[:], in_to_replace=picks[:], in_values=lg[:], imm_value=-NEG)\
                    .then_inc(pick_done.sem, 1)
                pick_done.wait(dve, row, 2)
                ex_ready.wait(dve, row)
                nc.vector.scalar_tensor_tensor(out=esel[:], in0=picked[:, 0:EXPERTS], scalar=-NEG, in1=ex[:],
                                               op0=ALU.is_equal, op1=ALU.mult).then_inc(sel_done.sem, 1)
                sel_done.wait(dve, row, 1)
                nc.vector.reduce_sum(esum[:], esel[:], X).then_inc(sel_done.sem, 1)
                sel_done.wait(dve, row, 2)
                nc.vector.reciprocal(erec[:], esum[:]).then_inc(sel_done.sem, 1)
                sel_done.wait(dve, row, 3)
                nc.vector.tensor_scalar(cw[row.par][:, 0:EXPERTS], esel[:], erec[:], SILU, ALU.mult, ALU.mult)\
                    .then_inc(cw_ready.sem, 1)

            def gate(dve, row, c):
                tanh_done.wait(dve, row, c + 1)
                if c == 0:
                    inner_done.wait(dve, row, back=1)
                else:
                    inner_done.wait(dve, row, c)
                n = width(c)
                nc.vector.scalar_tensor_tensor(out=ga[:, 0:n], in0=th[:, 0:n], scalar=1.0, in1=pg[:, 0:n],
                                               op0=ALU.add, op1=ALU.mult).then_inc(gate_done.sem, 1)

            def turn(dve, row, c):
                inner_hi.wait(dve, row, c + 1)
                nc.vector.tensor_tensor(hT[1][:].rearrange("p t n -> p (t n)"), ph[:, 0:CHUNK],
                                        hT[0][:].rearrange("p t n -> p (t n)"), ALU.subtract)\
                    .then_inc(inner_lo.sem, 1)

            def up(dve, row, c):
                gate_done.wait(dve, row, c + 1)
                up_ready.wait(dve, row, c + 1)
                if c == 0:
                    inner_T.wait(dve, row, back=1)
                    cw_ready.wait(dve, row, 1)
                else:
                    inner_T.wait(dve, row, c)
                    if c == SHARED // CHUNK:
                        cw_ready.wait(dve, row)
                for lo, hi, e in segments(c):
                    last = nc.vector.scalar_tensor_tensor(
                        out=hh[:, lo:hi], in0=pu[:, lo:hi], scalar=cw[row.par][:, e:e + 1],
                        in1=ga[:, lo:hi], op0=ALU.mult, op1=ALU.mult)
                last.then_inc(inner_done.sem, 1)

            def finish(dve, row):
                down_done.wait(dve, row)
                nc.vector.scalar_tensor_tensor(out=x2[row.par][:], in0=pacc[:, 0:E], scalar=1.0 / WS,
                                               in1=x2[row.par][:], op0=ALU.mult, op1=ALU.add)\
                    .then_inc(y_ready.sem, 1)

            nc.vector.memset(v_sb[0][:, :, HD:HD + 1], 1.0).then_inc(s_once, 1)
            nc.vector.memset(v_sb[1][:, :, HD:HD + 1], 0.0).then_inc(s_once, 1)
            nc.vector.memset(lg[:, EXPERTS:], NEG).then_inc(s_once, 1)
            nc.vector.memset(picks[:, TOP:], NEG).then_inc(s_once, 1)
            dve.wait_ge(s_once, 4)
            dve.wait_ge(s_const, NCONST)
            nc.vector.tensor_copy(id_b[:], id_sb[:]).then_inc(s_once, 1)
            nc.vector.tensor_copy(causal_b[:], causal_sb[:]).then_inc(s_once, 1)
            nc.vector.tensor_scalar(skip64[:], skip_sb[:], WS, None, ALU.mult).then_inc(s_once, 1)
            for kc in range(KC):
                dve.wait_ge(s_wa_hi, kc + 1)
                nc.vector.scalar_tensor_tensor(out=wa[1][:, kc, :], in0=stage_a[:, kc * AW:(kc + 1) * AW],
                                               scalar=WS, in1=wa[0][:, kc, :], op0=ALU.mult,
                                               op1=ALU.subtract).then_inc(s_wa_lo, 1)

            def split_toeplitz(dve):
                dve.wait_ge(s_t_hi, 1)
                nc.vector.scalar_tensor_tensor(out=toep_w[1][:].rearrange("p g c n -> p (g c n)"), in0=scratch[:],
                                               scalar=WS, in1=toep_w[0][:].rearrange("p g c n -> p (g c n)"),
                                               op0=ALU.mult, op1=ALU.subtract).then_inc(s_t_lo, 1)

            def prepare(dve, u):
                if u == TOEP_AT:
                    split_toeplitz(dve)
                c, n = divmod(u, UNITS)
                dve.wait_ge(s_w_hi, u + 1)
                nc.vector.scalar_tensor_tensor(out=unit_of(1, c, n), in0=stage[:, u % RING], scalar=WS,
                                               in1=unit_of(0, c, n), op0=ALU.mult, op1=ALU.subtract)\
                    .then_inc(s_w_lo, 1)

            pieces = {0: [(ATT, norm1[0])],
                      0.3: [(ATT, norm1[1]), (MIX, normalise), (MOE, choose)], 0.6: [(MIX, lhs_split(1))],
                      1.3: [(ATT, lhs_split(0)), (MIX, residual1), (MIX, norm2[0])], 2: [(MIX, norm2[1])],
                      2.3: [(ATT, rope(0)), (ATT, rope(1)), (ATT, mask_keys)],
                      3: [(ATT, v_bias)],
                      3.3: [(ATT, split_v), (ATT, row_max(0)), (ATT, row_max(1))],
                      3.6: [(MIX, skip_sum), (MIX, gate_conv(0, 0))], 4: [(MIX, gate_conv(0, 1))],
                      4.3: [(ATT, row_max(2)), (ATT, row_max(3))],
                      4.6: [(MIX, gate_conv(1, 0))], 5: [(MIX, gate_conv(1, 1))],
                      5.3: [(ATT, split_probs(0)), (ATT, split_probs(1))],
                      5.6: [(MIX, residual2), (MIX, norm3[0])], 6: [(MIX, norm3[1])],
                      6.3: [(ATT, split_probs(2)), (MIX, moe_x_lo), (ATT, split_probs(3))],
                      6.6: [(MIX, logits), (MIX, top)]}
            steps(dve, pieces, gate, turn, up, none, finish, prepare=prepare)

        @block.gpsimd
        def _(pool):
            def add_bias(pool, row):
                pool.wait_ge(s_x[row.par], row.half * 16 + 16)
                x1_ready.wait(pool, row, back=1)
                nc.gpsimd.tensor_tensor(xb[:], x_sb[row.par][:], bo_sb[:], ALU.add).then_inc(xb_ready.sem, 1)

            def rope_sin(side):
                def piece(pool, row):
                    qk_biased.wait(pool, row, side + 1)
                    roped.wait(pool, row, side + 1, back=1)
                    sin = trig_sb[:, side, 1:2, :].broadcast_to([P, 2, P])
                    nc.gpsimd.tensor_tensor(rs[:, side], qkb[:, 4 * side + 2:4 * side + 4, :], sin, ALU.mult)\
                        .then_inc(sin_done.sem, 1)
                return piece

            def products_kv(half):
                def piece(pool, row):
                    vc_ready.wait(pool, row)
                    if isinstance(row.b, int) and row.b == 0:
                        pool.wait_ge(s_t_hi, 1)
                        pool.wait_ge(s_t_lo, 1)
                    G2 = GROUPS // 2
                    cols = slice(half * 64, half * 64 + 64)
                    for c in range(KC):
                        vT = vcT[:, 0, c, cols].rearrange("p (h a i) -> p h a i", a=1, i=SIDE)
                        cT = vcT[:, 1, c, cols].rearrange("p (h j a) -> p h j a", a=1, j=SIDE)
                        last = nc.gpsimd.tensor_tensor(
                            kv[:, c, half * G2:(half + 1) * G2, :].rearrange("p h (j i) -> p h j i", i=SIDE),
                            cT.broadcast_to([P, G2, SIDE, SIDE]), vT.broadcast_to([P, G2, SIDE, SIDE]), ALU.mult)
                    last.then_inc(kv_ready.sem, 1)
                return piece

            def split_kv(half):
                def piece(pool, row):
                    kv_hi.wait(pool, row, half + 1)
                    groups = slice(8 * half, 8 * half + 8)
                    nc.gpsimd.tensor_tensor(kvh[1][:, :, groups, :], kv[:, :, groups, :], kvh[0][:, :, groups, :],
                                            ALU.subtract).then_inc(kv_lo.sem, 1)
                return piece

            def skip_products(pool, row):
                sk_sum.wait(pool, row, back=1)
                nc.gpsimd.tensor_tensor(sk1[:], vcT[:, 0], vcT[:, 1], ALU.mult).then_inc(sk_mul.sem, 1)
                sk_mul.wait(pool, row, 1)
                nc.gpsimd.tensor_tensor(sk2[:], sk1[:],
                                        skip64[:].rearrange("p (a n) -> p a n", a=1).broadcast_to([P, KC, P]),
                                        ALU.mult).then_inc(sk_mul.sem, 1)

            def skip_out(pool, row):
                sk_sum.wait(pool, row)
                o2_ready.wait(pool, row, back=1)
                nc.gpsimd.tensor_tensor(skc[:].rearrange("p c (g j) -> p (c g) j", j=SIDE),
                                        vcT[:, 1].rearrange("p c (g j) -> p (c g) j", j=SIDE),
                                        sks[:].rearrange("p c (g a) -> p (c g) a", a=1)
                                        .broadcast_to([P, KC * GROUPS, SIDE]), ALU.mult).then_inc(sk_out.sem, 1)

            def conv_out(pool, row):
                gsum.wait(pool, row)
                sk_out.wait(pool, row)
                o2_T.wait(pool, row, back=1)
                nc.gpsimd.tensor_tensor(o2f[:], o2[:], skc[:], ALU.add).then_inc(o2_ready.sem, 1)

            def root(n):
                def piece(pool, row):
                    ln_step[n].wait(pool, row)
                    nc.gpsimd.tensor_tensor(rstd[n][:], var[n][:], minus_half[:], ALU.pow)\
                        .then_inc(rstd_ready[n].sem, 1)
                return piece

            nc.gpsimd.memset(minus_half[:], -0.5).then_inc(s_half, 1)
            pool.wait_ge(s_half, 1)
            pool.wait_ge(s_once, 7)
            pool.wait_ge(s_const, NCONST)
            pieces = {0: [(ATT, root(0))], 1.3: [(MIX, root(1))],
                      2.3: [(MIX, products_kv(0)), (ATT, rope_sin(0)), (ATT, rope_sin(1)), (MIX, products_kv(1)),
                            (MIX, split_kv(0)), (MIX, split_kv(1)), (MIX, skip_products)],
                      4: [(MIX, skip_out)], 5: [(MIX, conv_out)], 5.6: [(MIX, root(2)), (ATT, add_bias)]}
            steps(pool, pieces, none, none, none, none, none)


def rope_tables():
    pos = np.arange(P, dtype=np.float32)[:, None]
    exps = -np.arange(0, HD, 2, dtype=np.float32) / np.float32(HD)
    thetas = np.repeat(np.power(np.float32(10000.0), exps), 2)
    angles = (pos * thetas[None, :]).astype(np.float32)
    sign = np.where(np.arange(HD) % 2 == 0, -1.0, 1.0)
    cos = np.cos(angles).T
    sin = np.sin(angles).T * sign[:, None]
    both = np.stack([np.tile(cos, (P // HD, 1)), np.tile(sin, (P // HD, 1))], axis=1).astype(np.float32)
    return np.stack([both * np.float32(HD ** -0.5), both], axis=1)


def constants():
    at = np.arange(P)
    return {
        "trig": rope_tables(),
        "causal": np.where(at[None, :] > at[:, None], NEG, 0.0).astype(np.float32),
        "ident": np.eye(P, dtype=np.float32),
        "halves": np.stack([(at // HD) % 2 == 0, (at // HD) % 2 == 1], axis=1).astype(np.float32),
    }


def by_rows(w):
    return w.reshape(KC, P, -1).transpose(1, 0, 2)


def attention_weights(Wq, Wk, Wv, Wo, gate_w, gate_vec):
    swap = np.arange(E) ^ 1
    pad = np.zeros((E, AW - R0 - NR), np.float32)
    w = np.concatenate([Wq, Wq[:, swap], Wk, Wk[:, swap], Wv, Wo, gate_w.T, gate_vec.T, pad], axis=1)
    return by_rows(w).reshape(P, KC * AW)


def expert_weights(egu, ed, sgu, sd):
    gates = np.concatenate([sgu[:SHARED], egu[:, :INTER].reshape(-1, E)])
    ups = np.concatenate([sgu[SHARED:], egu[:, INTER:].reshape(-1, E)])
    downs = np.concatenate([sd.T, ed.transpose(0, 2, 1).reshape(-1, E)])
    gates, ups, downs = (np.concatenate([w, np.zeros((NCHUNK * CHUNK - INNER, E), np.float32)])
                         for w in (gates, ups, downs))
    gu = np.stack([gates.reshape(NCHUNK, CHUNK, KC, P), ups.reshape(NCHUNK, CHUNK, KC, P)])
    gu = gu.transpose(1, 3, 4, 0, 2).reshape(NCHUNK, KC, P, UNIT)
    dn = downs.reshape(NCHUNK, DT, P, E).transpose(0, 2, 1, 3).reshape(NCHUNK, 1, P, UNIT)
    return np.concatenate([gu, dn], axis=1).reshape(NCHUNK * UNITS, P, UNIT)


def toeplitz(k):
    padded = np.concatenate([np.zeros((GROUPS, P - 1), np.float32), k], axis=1)
    at = P - 1 + np.arange(2 * P)[None, :] - np.arange(P)[:, None]
    return padded[:, at].transpose(1, 0, 2).reshape(P, GROUPS, 2, P)


def bias_columns(bq, bk):
    swap = np.arange(E) ^ 1
    return np.stack([b.reshape(KC, P)[c] for b in (bq, bq[swap], bk, bk[swap]) for c in range(KC)], axis=1)


def kernel(**inputs):
    import concourse.bacc as bacc
    from concourse.bass_utils import run_bass_kernel_spmd

    a = {n: np.asarray(v) for n, v in inputs.items()}
    arrays = {
        "x": a["x"], "ctx_in": a["ctx_2048"],
        "w_attn": attention_weights(a["L0_attn_Wq"], a["L0_attn_Wk"], a["L0_attn_Wv"], a["L0_attn_Wo"],
                                    a["L0_ffn_gate_w"], a["L0_ffn_shared_gate_vec"]),
        "w_moe": expert_weights(a["L0_ffn_expert_gate_up"], a["L0_ffn_expert_down"],
                                a["L0_ffn_shared_gate_up"], a["L0_ffn_shared_down"]),
        "toep": toeplitz(a["L0_xattn_k"]),
        "bias_qk": bias_columns(a["L0_attn_bq"], a["L0_attn_bk"]),
        "bias_v": a["L0_attn_bv"], "bias_o": a["L0_attn_bo"], "skip": a["fside_S2_0"],
        **constants(),
    }
    nc = bacc.Bacc("TRN2", target_bir_lowering=False, num_devices=1)
    args = {}
    arrays = {f"in_{n}": np.ascontiguousarray(v) for n, v in arrays.items()}
    for n, v in arrays.items():
        args[n[3:]] = nc.dram_tensor(n, v.shape, mybir.dt.from_np(v.dtype), kind="ExternalInput").ap()
    out = nc.dram_tensor("out_y", a["x"].shape, F32, kind="ExternalOutput").ap()
    build(nc, out=out, **args)
    r = run_bass_kernel_spmd(nc, [arrays], core_ids=[0])
    return r.results[0]["out_y"]
```

```python
from contextlib import ExitStack

import numpy as np
import concourse.bass as bass
from concourse import mybir

ALU = mybir.AluOpType
ACT = mybir.ActivationFunctionType
F32 = mybir.dt.float32
F16 = mybir.dt.float16
BF16 = mybir.dt.bfloat16
X = mybir.AxisListType.X

P = 128
E = 256
KC = E // P
HEADS, HD = 16, 16
GROUPS, SIDE = 16, 8
EXPERTS, TOP, INTER, SHARED = 16, 4, 176, 704
CHUNK = 512
INNER = SHARED + EXPERTS * INTER
NCHUNK = -(-INNER // CHUNK)
DT = CHUNK // P
UNIT = 2 * CHUNK
UNITS = KC + DT * E // UNIT
RING = 4
WS = 64.0
SILU = 0.5 / (WS * WS)
EPS = 1e-5
NEG = -1e30
V0, O0, R0, NR = 2 * E, 3 * E, 4 * E, EXPERTS + 1
VW = 2 * HD + 1
ROWS = 64
AW = R0 + 20


def width(c):
    return min(CHUNK, INNER - c * CHUNK)


def tiles(c):
    return [min(P, width(c) - t) for t in range(0, width(c), P)]


def segments(c):
    bounds = [(0, SHARED, EXPERTS)] + [(SHARED + e * INTER, SHARED + (e + 1) * INTER, e) for e in range(EXPERTS)]
    at, end = c * CHUNK, c * CHUNK + width(c)
    return [(max(lo, at) - at, min(hi, end) - at, e) for lo, hi, e in bounds if lo < end and hi > at]


class Row:

    def __init__(self, b, half, par):
        self.b, self.half, self.par = b, half, par


def numbered(b):
    return Row(b, b // 2, b % 2)


class Signal:

    def __init__(self, sem, per):
        self.sem, self.per = sem, per

    def value(self, row, k=None, back=0):
        k = self.per if k is None else k
        return row.b * self.per + (k - back * self.per)

    def wait(self, eng, row, k=None, back=0):
        if isinstance(row.b, int) and row.b < back:
            return
        eng.wait_ge(self.sem, self.value(row, k, back))


def build(nc, x, ctx_in, w_attn, w_moe, toep, bias_qk, bias_v, bias_o, skip,
          trig, causal, ident, out):
    NB = x.shape[0]
    stack = ExitStack()
    with stack:
        def sb(name, shape, dt=F32):
            return stack.enter_context(nc.sbuf_tensor(name, shape, dt))

        def sem(name):
            return stack.enter_context(nc.semaphore(name))

        def signal(name, per=1):
            return Signal(sem(name), per)

        wa = [sb(f"w_attn_{n}", [P, KC, AW], F16) for n in ("hi", "lo")]
        wgu = [sb(f"w_gate_up_{n}", [P, NCHUNK, KC, 2, CHUNK], F16) for n in ("hi", "lo")]
        wd = [sb(f"w_down_{n}", [P, NCHUNK, DT, E], F16) for n in ("hi", "lo")]
        toep_w = [sb(f"toeplitz_{n}", [P, GROUPS, 2, P], F16) for n in ("hi", "lo")]
        bqk_sb = sb("bias_qk_sb", [P, 2 * E])
        bv_sb = sb("bias_v_sb", [P, E])
        bo_sb = sb("bias_o_sb", [P, E])
        skip_sb = sb("skip_sb", [P, P])
        skip64 = sb("skip_scaled_once", [P, P])
        trig_sb = sb("trig_sb", [P, 2, 2, HD])
        causal_sb = sb("causal_sb", [P, P])
        causal_b = sb("causal_bf16", [P, P], BF16)
        id_b = sb("identity_bf16", [P, P], BF16)
        id_sb = sb("identity", [P, P])
        id_h = sb("identity_fp16", [P, P], F16)
        stage = sb("stage_moe", [P, RING, UNIT])
        x_sb = [sb(f"x_sb{i}", [P, E]) for i in range(2)]
        c_sb = [sb(f"ctx_t_sb{i}", [P, KC, P]) for i in range(2)]
        xb = sb("x_plus_bias", [P, E])
        st6 = [sb(f"ln_stats{n}", [P, 6]) for n in range(3)]
        mv = [sb(f"ln_mean_var{n}", [P, 2]) for n in range(3)]
        var = [sb(f"ln_var{n}", [P, 1]) for n in range(3)]
        rstd = [sb(f"ln_rstd{n}", [P, 1]) for n in range(3)]
        xn = [sb(f"x_norm{n}", [P, E]) for n in range(3)]
        minus_half = sb("minus_half", [P, 1])
        tT = [sb(f"lhs_t_{n}", [P, KC, P], F16) for n in ("hi", "lo")]
        qkb = sb("qk_biased", [P, 2, HEADS, HD])
        qk = sb("qk_cos_then_roped", [P, 2, HEADS, HD])
        rs = sb("rope_sin", [P, 2, HEADS, HD])
        terms = [sb(f"{n}_terms", [P, HEADS, ROWS], F16) for n in "qk"]
        termT = [sb(f"{n}_terms_t", [P, HEADS // 2, P], F16) for n in "qk"]
        v_f = sb("v_biased", [P, HEADS, HD])
        v_cat = sb("v_hi_ones_lo", [P, HEADS, VW], F16)
        sm = sb("probs", [P, 4, 4, P])
        pT = [sb(f"probs_t_{n}", [P, 4, 4, P], F16) for n in ("hi", "lo")]
        mx = sb("row_neg_max", [P, 4, 4])
        rsum = sb("softmax_recip", [P, HEADS])
        o_sb = sb("attn_out", [P, E])
        x1 = sb("x1", [P, E])
        vT = sb("v_t", [P, KC, P])
        scratch = sb("scratch", [P, 2 * GROUPS * P])
        stage_a = scratch[:, 0:KC * AW]
        kv = scratch[:, 0:2048].rearrange("p (c h n) -> p c h n", c=KC, h=GROUPS)
        z = scratch[:, 2048:3072]
        sk1, sk2, o2, o2f = (scratch[:, n:n + E].rearrange("p (c n) -> p c n", c=KC)
                             for n in range(3072, 4096, E))
        kvh = [sb(f"kv_{n}", [P, KC, GROUPS, SIDE * SIDE], F16) for n in ("hi", "lo")]
        sks = sb("skip_sum", [P, KC, GROUPS])
        skc = sb("skip_out", [P, KC, P])
        places = stage[:].rearrange("p r n -> p (r n)")
        late = iter(np.cumsum([0, E, E, CHUNK, CHUNK, CHUNK, CHUNK]).tolist())

        def take(n, dt=F32):
            at = next(late)
            return places[:, at:at + n] if dt == F32 else places[:, at:at + n].bitcast(dt)

        x2 = [sb("x2_0", [P, E]), take(E)]
        xT_odd = take(E, F16).rearrange("p (s c n) -> p s c n", s=2, c=KC)
        xT = [[sb(f"moe_x_t_{n}", [P, KC, P], F16) for n in ("hi", "lo")], [xT_odd[:, 0], xT_odd[:, 1]]]
        lg = sb("logits", [P, EXPERTS + 8 - TOP])
        top8 = sb("top8", [P, 8])
        picks = sb("picks", [P, 8])
        picked = sb("picked", [P, EXPERTS + 8 - TOP])
        lmax = sb("logit_neg_max", [P, 1])
        ex = sb("router_exp", [P, EXPERTS])
        gth = sb("gate_tanh", [P, 1])
        esel = sb("router_sel", [P, EXPERTS])
        esum = sb("router_sum", [P, 1])
        erec = sb("router_recip", [P, 1])
        cw = [sb(f"expert_weight{i}", [P, NR]) for i in range(2)]
        th = take(CHUNK)
        ga = take(CHUNK)
        hh = take(CHUNK)
        hT_both = take(CHUNK, F16).rearrange("p (s t n) -> p s t n", s=2, t=DT)
        hT = [hT_both[:, 0], hT_both[:, 1]]

        def bank(name):
            return stack.enter_context(nc.psum_tensor(name, [P, 512], F32))

        pg, pu, ph, pacc = bank("ps_gate"), bank("ps_up"), bank("ps_inner_t"), bank("ps_out")
        pf = stack.enter_context(nc.psum_tensor("ps_front", [P, 4, 512], F32))

        s_const = sem("const_loaded")
        s_wa = [sem(f"attn_weights_loaded{i}") for i in range(KC)]
        s_toep = sem("toeplitz_loaded")
        s_stage = [sem(f"moe_weights_loaded{i}") for i in range(RING)]
        s_x = [sem(f"x_loaded{i}") for i in range(2)]
        s_c = [sem(f"ctx_loaded{i}") for i in range(2)]
        s_y = [sem(f"y_stored{i}") for i in range(2)]
        s_wa_hi, s_wa_lo = sem("attn_hi_done"), sem("attn_lo_done")
        s_t_hi, s_t_lo = sem("toeplitz_hi_done"), sem("toeplitz_lo_done")
        s_w_hi, s_w_lo = sem("moe_hi_done"), sem("moe_lo_done")
        s_once = sem("constants_set")
        s_half = sem("minus_half_set")
        s_tables = sem("tables_loaded")

        ln_step = [signal(f"ln{n}_step", 3) for n in range(3)]
        rstd_ready = [signal(f"ln{n}_rstd") for n in range(3)]
        normed = [signal(f"ln{n}_done") for n in range(3)]
        xb_ready = signal("x_plus_bias_ready")
        xn_T = signal("xn_transposed")
        lhs_hi = signal("lhs_hi", 2)
        lhs_lo = signal("lhs_lo", 2)
        qk_ready = signal("qk_projected")
        v_ready = signal("v_projected")
        qk_biased = signal("qk_biased")
        v_done = signal("v_done")
        v_hi = signal("v_hi")
        v_lo = signal("v_lo")
        cos_done = signal("cos_done")
        sin_done = signal("sin_done")
        roped = signal("roped")
        term_hi = signal("qk_term_hi", 2)
        term_lo = signal("qk_term_lo", 2)
        terms_T = signal("qk_transposed", 2)
        qT_ready = signal("q_t_ready")
        kT_ready = signal("k_t_ready")
        scored = signal("scored", 2)
        maxed = signal("maxed", 4)
        exped = signal("exped", 4)
        probs_T = signal("probs_transposed", 4)
        pT_hi = signal("probs_t_hi", 4)
        pT_lo = signal("probs_t_lo", 4)
        av_ready = signal("av_ready")
        recip_done = signal("recip_done")
        o_summed = signal("attn_out_summed", 2)
        o_ready = signal("attn_out_ready")
        o_T = signal("attn_out_transposed")
        wo_ready = signal("wo_ready")
        x1_ready = signal("x1_ready")
        v_T = signal("v_transposed")
        vT_ready = signal("v_t_ready")
        kv_ready = signal("kv_ready", 2)
        kv_hi = signal("kv_hi", 2)
        kv_lo = signal("kv_lo", 2)
        sk_mul = signal("skip_multiplied", 2)
        sk_sum = signal("skip_summed")
        sk_out = signal("skip_out_done")
        conv_ready = signal("conv_ready", 2)
        gated = signal("conv_gated", 4)
        gsum = signal("conv_summed", 4)
        o2_ready = signal("conv_out_ready")
        o2_T = signal("conv_out_transposed")
        x2_ready = signal("x2_ready")
        xn3_T = signal("xn3_transposed")
        xT_hi = signal("moe_x_hi")
        xT_lo = signal("moe_x_lo")
        routed = signal("router_logits")
        lg_ready = signal("logits_ready")
        lmax_ready = signal("logit_max_ready")
        gth_ready = signal("shared_gate_tanh_ready")
        ex_ready = signal("router_exp_ready")
        top_ready = signal("top8_ready")
        pick_done = signal("pick_done", 2)
        sel_done = signal("select_done", 3)
        cw_ready = signal("expert_weight_ready", 2)

        NC = NCHUNK
        gate_ready = signal("gate_ready", NC)
        up_ready = signal("up_ready", NC)
        tanh_done = signal("tanh_done", NC)
        gate_done = signal("gate_done", NC)
        inner_done = signal("inner_done", NC)
        inner_T = signal("inner_transposed", NC)
        inner_hi = signal("inner_hi", NC)
        inner_lo = signal("inner_lo", NC)
        down_done = signal("down_done", NC)
        y_ready = signal("y_ready")

        ring = lambda g: pf[:, g, :]

        def products(first, last):
            terms = ((0, 0), (0, 1), (1, 0))
            return [(a, b, first and n == 0, last and n == 2) for n, (a, b) in enumerate(terms)]

        ATT, MIX, MOE = 0, 1, 2

        def step(eng, att, mix, moe, prev, pieces, gate, turn, up, down, finish, fill=None):
            rows = (att, mix, moe)

            def run(at):
                if fill is not None:
                    fill(at)
                for which, piece in pieces.get(at, ()):
                    if rows[which] is not None:
                        piece(eng, rows[which])

            for c in range(NC):
                before = (moe, c - 1) if c > 0 else (prev, NC - 1)
                if before[0] is not None:
                    turn(eng, *before)
                run(c)
                if moe is not None:
                    gate(eng, moe, c)
                    up(eng, moe, c)
                run(c + .3)
                if before[0] is not None:
                    down(eng, *before)
                    if c == 0:
                        finish(eng, prev)
                run(c + .6)
                run(c + .8)

        def steps(eng, *fns, prepare=None, plans=({}, {})):
            def fill(plan):
                return lambda at: [prepare(eng, u) for u in plan.get(at, ())]

            step(eng, numbered(0), None, None, None, *fns, fill=fill(plans[0]))
            step(eng, numbered(1), numbered(0), None, None, *fns, fill=fill(plans[1]))
            step(eng, numbered(2), numbered(1), numbered(0), None, *fns)
            step(eng, numbered(3), numbered(2), numbered(1), numbered(0), *fns)
            with eng.Fori(0, (NB - 4) // 2) as i:
                step(eng, Row(2 * i + 4, i + 2, 0), Row(2 * i + 3, i + 1, 1), Row(2 * i + 2, i + 1, 0),
                     Row(2 * i + 1, i, 1), *fns)
                step(eng, Row(2 * i + 5, i + 2, 1), Row(2 * i + 4, i + 2, 0), Row(2 * i + 3, i + 1, 1),
                     Row(2 * i + 2, i + 1, 0), *fns)
            step(eng, None, numbered(NB - 1), numbered(NB - 2), numbered(NB - 3), *fns)
            step(eng, None, None, numbered(NB - 1), numbered(NB - 2), *fns)
            turn, down, finish = fns[2], fns[4], fns[5]
            turn(eng, numbered(NB - 1), NC - 1)
            down(eng, numbered(NB - 1), NC - 1)
            finish(eng, numbered(NB - 1))

        NCONST = 16 * 7
        TOEP, ATTN = -1, -2

        def unit_of(half, c, n):
            if n < KC:
                return wgu[half][:, c, n].rearrange("p s n -> p (s n)")
            return wd[half][:, c].rearrange("p t n -> p (t n)")

        def wait_apart(eng, *waits):
            values = [v if isinstance(v, int) else eng.to_reg(v) for _, v in waits]
            eng.wait_ge(s_const, NCONST)
            for (semaphore, _), value in zip(waits, values):
                eng.wait_ge(semaphore, value)

        none = lambda *a: None
        block = stack.enter_context(nc.Block())

        @block.sync
        def _(sp):
            def load_x(row):
                if not (isinstance(row.b, int) and row.b < 2):
                    wait_apart(sp, (normed[0].sem, normed[0].value(row, back=2)),
                               (xb_ready.sem, xb_ready.value(row, back=2)))
                sp.dma_start(x_sb[row.par][:], x[row.b]).then_inc(s_x[row.par], 16)

            def load_ctx(row):
                if not (isinstance(row.b, int) and row.b < 2):
                    wait_apart(sp, (o2_ready.sem, o2_ready.value(row, back=2)))
                sp.dma_start(c_sb[row.par][:], ctx_in[row.b]).then_inc(s_c[row.par], 16)

            def store_row(row):
                wait_apart(sp, (y_ready.sem, y_ready.value(row)))
                sp.dma_start(out[row.b], x2[row.par][:]).then_inc(s_y[row.par], 16)

            load_x(numbered(0))
            def load_attention_weights(kc):
                cols = slice(kc * AW, (kc + 1) * AW)
                sp.dma_start(stage_a[:, cols], w_attn[:, cols]).then_inc(s_wa[kc], 16)

            load_attention_weights(0)
            for dst, src in ((id_sb, ident), (trig_sb, trig), (causal_sb, causal)):
                sp.dma_start(dst[:], src).then_inc(s_const, 16)
            for dst, src in ((bqk_sb, bias_qk), (bv_sb, bias_v), (bo_sb, bias_o), (skip_sb, skip)):
                sp.dma_start(dst[:], src.partition_broadcast(P)).then_inc(s_const, 16)
            load_attention_weights(1)
            load_x(numbered(1))
            for r in range(2):
                load_ctx(numbered(r))
            for u in range(NC * UNITS):
                if u == RING:
                    sp.wait_ge(s_wa_lo, KC)
                    sp.dma_start(scratch[:], toep).then_inc(s_toep, 16)
                if u >= RING:
                    sp.wait_ge(s_w_lo, u - RING + 1)
                sp.dma_start(stage[:, u % RING], w_moe[u]).then_inc(s_stage[u % RING], 16)
            load_x(numbered(2))
            load_x(numbered(3))
            load_ctx(numbered(2))
            for r in range(2):
                store_row(numbered(r))
                load_x(numbered(r + 4))
                load_ctx(numbered(r + 3))
            with sp.Fori(0, (NB - 6) // 2) as i:
                store_row(Row(2 * i + 2, i + 1, 0))
                load_x(Row(2 * i + 6, i + 3, 0))
                load_ctx(Row(2 * i + 5, i + 2, 1))
                store_row(Row(2 * i + 3, i + 1, 1))
                load_x(Row(2 * i + 7, i + 3, 1))
                load_ctx(Row(2 * i + 6, i + 3, 0))
            store_row(numbered(NB - 4))
            load_ctx(numbered(NB - 1))
            for r in range(NB - 3, NB):
                store_row(numbered(r))
            for par in range(2):
                sp.wait_ge(s_y[par], 16 * (NB // 2))

        @block.tensor
        def _(pe):
            def t_norm(pe, row):
                normed[0].wait(pe, row)
                lhs_lo.wait(pe, row, back=1)
                for c in range(KC):
                    last = nc.tensor.transpose(ring(3)[:, c * P:(c + 1) * P], xn[0][:, c * P:(c + 1) * P], id_sb[:])
                last.then_inc(xn_T.sem, 1)

            def project_qk(pe, row):
                lhs_hi.wait(pe, row, 1)
                lhs_lo.wait(pe, row, 1)
                if isinstance(row.b, int) and row.b == 0:
                    pe.wait_ge(s_wa_hi, KC)
                    pe.wait_ge(s_wa_lo, KC)
                x1_ready.wait(pe, row, back=1)
                for kc in range(KC):
                    for a, b, first, end in products(kc == 0, kc == KC - 1):
                        last = nc.tensor.matmul(ring(2), tT[a][:, kc, :], wa[b][:, kc, 0:2 * E],
                                                start=first, stop=end)
                last.then_inc(qk_ready.sem, 1)

            def project_v(pe, row):
                lhs_hi.wait(pe, row, 1)
                lhs_lo.wait(pe, row, 1)
                for kc in range(KC):
                    for a, b, first, end in products(kc == 0, kc == KC - 1):
                        last = nc.tensor.matmul(ring(3)[:, 0:E], tT[a][:, kc, :], wa[b][:, kc, V0:V0 + E],
                                                start=first, stop=end)
                last.then_inc(v_ready.sem, 1)

            def t_terms(side):
                def piece(pe, row):
                    term_hi.wait(pe, row, side + 1)
                    term_lo.wait(pe, row, side + 1)
                    qk_biased.wait(pe, row)
                    v_done.wait(pe, row)
                    to = ring(2 + side).bitcast(F16)
                    for j in range(HEADS // 2):
                        two = terms[side][:, 2 * j:2 * j + 2, :].rearrange("p h r -> p (h r)")
                        last = nc.tensor.transpose(to[:, j * P:(j + 1) * P], two, id_h[:])
                    last.then_inc(terms_T.sem, 1)
                return piece

            def scores(half):
                def piece(pe, row):
                    if half == 0:
                        qT_ready.wait(pe, row)
                        kT_ready.wait(pe, row)
                    else:
                        exped.wait(pe, row, 2)
                    for bank in (2, 3):
                        nc.tensor.matmul(ring(bank).rearrange("p (s n) -> p s n", n=P), id_b[:],
                                         causal_b[:].rearrange("p (a n) -> p a n", a=1).broadcast_to([P, 4, P]),
                                         start=True, stop=False, skip_group_check=True)
                    for n in range(8):
                        h = 8 * half + n
                        rows = slice(h % 2 * ROWS, h % 2 * ROWS + 3 * HD)
                        last = nc.tensor.matmul(ring(2 + n % 2)[:, n // 2 * P:(n // 2 + 1) * P],
                                                termT[0][rows, h // 2, :], termT[1][rows, h // 2, :],
                                                start=False, stop=True, skip_group_check=True)
                    last.then_inc(scored.sem, 1)
                return piece

            def t_probs(g):
                def piece(pe, row):
                    exped.wait(pe, row, g + 1)
                    if g < 2:
                        exped.wait(pe, row, g + 3)
                    else:
                        pT_lo.wait(pe, row, g - 1)
                    for s in range(4):
                        last = nc.tensor.transpose(ring(2 + g % 2)[:, s * P:(s + 1) * P], sm[:, g, s, :], id_sb[:])
                    last.then_inc(probs_T.sem, 1)
                return piece

            def attend(pe, row):
                pT_hi.wait(pe, row)
                pT_lo.wait(pe, row)
                v_hi.wait(pe, row)
                v_lo.wait(pe, row)
                for h in range(HEADS):
                    g, s = 2 * (h // 8) + h % 2, h % 8 // 2
                    to = ring(2 + h // 8)[:, h % 8 * VW:(h % 8 + 1) * VW]
                    nc.tensor.matmul(to, pT[0][:, g, s, :], v_cat[:, h, :], start=True, stop=False,
                                     skip_group_check=True)
                    last = nc.tensor.matmul(to[:, 0:HD + 1], pT[1][:, g, s, :], v_cat[:, h, 0:HD + 1],
                                            start=False, stop=True, skip_group_check=True)
                last.then_inc(av_ready.sem, 1)

            def t_attn(pe, row):
                o_ready.wait(pe, row)
                for c in range(KC):
                    last = nc.tensor.transpose(ring(3)[:, c * P:(c + 1) * P], o_sb[:, c * P:(c + 1) * P], id_sb[:])
                last.then_inc(o_T.sem, 1)

            def out_proj(pe, row):
                lhs_hi.wait(pe, row, 2)
                lhs_lo.wait(pe, row, 2)
                for kc in range(KC):
                    for a, b, first, end in products(kc == 0, kc == KC - 1):
                        last = nc.tensor.matmul(ring(2)[:, 0:E], tT[a][:, kc, :], wa[b][:, kc, O0:O0 + E],
                                                start=first, stop=end)
                last.then_inc(wo_ready.sem, 1)

            def t_v(pe, row):
                normed[1].wait(pe, row)
                lg_ready.wait(pe, row, back=1)
                gth_ready.wait(pe, row, back=1)
                for c in range(KC):
                    last = nc.tensor.transpose(ring(0)[:, c * P:(c + 1) * P], xn[1][:, c * P:(c + 1) * P], id_sb[:])
                last.then_inc(v_T.sem, 1)

            def conv(half):
                def piece(pe, row):
                    kv_hi.wait(pe, row, half + 1)
                    kv_lo.wait(pe, row, half + 1)
                    if half == 0:
                        vT_ready.wait(pe, row)
                        xT_lo.wait(pe, row, back=1)
                        if isinstance(row.b, int) and row.b == 0:
                            pe.wait_ge(s_t_hi, 1)
                            pe.wait_ge(s_t_lo, 1)
                    else:
                        gated.wait(pe, row, 2)
                    for h in range(8 * half, 8 * half + 8):
                        to = ring(h // 4 % 2)[:, (h % 4) * P:(h % 4) * P + P]
                        for a, b, first, end in products(True, False):
                            nc.tensor.matmul(to.rearrange("p (c n) -> p c n", c=2), toep_w[a][:, h, 0, :],
                                             kvh[b][:, :, h, :], start=first, stop=end, skip_group_check=True)
                        for a, b, first, end in products(False, True):
                            last = nc.tensor.matmul(to[:, 64:128], toep_w[a][:, h, 1, :], kvh[b][:, 0, h, :],
                                                    start=first, stop=end, skip_group_check=True)
                    last.then_inc(conv_ready.sem, 1)
                return piece

            def t_conv(pe, row):
                o2_ready.wait(pe, row)
                gated.wait(pe, row)
                for c in range(KC):
                    last = nc.tensor.transpose(ring(0)[:, c * P:(c + 1) * P], o2f[:, c, :], id_sb[:])
                last.then_inc(o2_T.sem, 1)

            def t_norm3(pe, row):
                normed[2].wait(pe, row)
                for c in range(KC):
                    last = nc.tensor.transpose(ring(1)[:, c * P:(c + 1) * P], xn[2][:, c * P:(c + 1) * P], id_sb[:])
                last.then_inc(xn3_T.sem, 1)

            def router(pe, row):
                xT_hi.wait(pe, row)
                xT_lo.wait(pe, row)
                x2_ready.wait(pe, row)
                n = 0
                for kc in range(KC):
                    for a in range(2):
                        for b in range(2):
                            last = nc.tensor.matmul(ring(0)[:, 0:NR], xT[row.par][a][:, kc, :],
                                                    wa[b][:, kc, R0:R0 + NR], start=n == 0, stop=n == 7)
                            n += 1
                last.then_inc(routed.sem, 1)

            def half_product(bank, side, pe, row, c, ready):
                for kc in range(KC):
                    for a, b, first, end in products(kc == 0, kc == KC - 1):
                        last = nc.tensor.matmul(bank[:, 0:width(c)], xT[row.par][a][:, kc, :],
                                                wgu[b][:, c, kc, side, 0:width(c)], start=first, stop=end)
                last.then_inc(ready.sem, 1)

            def gate(pe, row, c):
                if c == 0:
                    xT_hi.wait(pe, row)
                    xT_lo.wait(pe, row)
                    gate_done.wait(pe, row, back=1)
                else:
                    gate_done.wait(pe, row, c)
                if isinstance(row.b, int) and row.b == 0 and c == 0:
                    pe.wait_ge(s_w_lo, NC * UNITS)
                    pe.wait_ge(s_w_hi, NC * UNITS)
                half_product(pg, 0, pe, row, c, gate_ready)

            def up(pe, row, c):
                if c == 0:
                    inner_done.wait(pe, row, back=1)
                else:
                    inner_done.wait(pe, row, c)
                half_product(pu, 1, pe, row, c, up_ready)

            def turn(pe, row, c):
                inner_done.wait(pe, row, c + 1)
                if c == 0:
                    inner_lo.wait(pe, row, back=1)
                else:
                    inner_lo.wait(pe, row, c)
                for t, n in enumerate(tiles(c)):
                    last = nc.tensor.transpose(ph[0:n, t * P:(t + 1) * P], hh[:, t * P:t * P + n], id_sb[:])
                last.then_inc(inner_T.sem, 1)

            def down(pe, row, c):
                inner_hi.wait(pe, row, c + 1)
                inner_lo.wait(pe, row, c + 1)
                if c == 0:
                    y_ready.wait(pe, row, back=1)
                for t, n in enumerate(tiles(c)):
                    for a, b, first, end in products(c == 0 and t == 0, c == NC - 1 and t == len(tiles(c)) - 1):
                        last = nc.tensor.matmul(pacc[:, 0:E], hT[a][0:n, t, :], wd[b][0:n, c, t, :],
                                                start=first, stop=end)
                last.then_inc(down_done.sem, 1)

            pe.wait_ge(s_const, NCONST)
            pe.wait_ge(s_once, 9)
            pieces = {0: [(MOE, router)], 0.3: [(MIX, attend)], 1: [(MIX, t_attn)], 1.3: [(MIX, out_proj), (ATT, t_norm)],
                      2.3: [(MIX, t_v), (ATT, project_qk), (ATT, project_v)],
                      3.3: [(ATT, t_terms(0)), (ATT, t_terms(1))], 3.6: [(ATT, scores(0)), (MIX, conv(0))],
                      4.3: [(ATT, scores(1))], 4.6: [(MIX, conv(1))],
                      5.3: [(ATT, t_probs(0)), (ATT, t_probs(1))], 5.6: [(MIX, t_conv)],
                      6.3: [(ATT, t_probs(2)), (MIX, t_norm3), (ATT, t_probs(3))]}
            steps(pe, pieces, gate, turn, up, down, none)

        @block.scalar
        def _(act):
            def lhs_split(n):
                def piece(act, row):
                    (xn_T, o_T)[n].wait(act, row)
                    if n == 0:
                        wo_ready.wait(act, row, back=1)
                    else:
                        v_ready.wait(act, row)
                    nc.scalar.activation(tT[0][:].rearrange("p c n -> p (c n)"), ring(3)[:, 0:E],
                                         ACT.Copy).then_inc(lhs_hi.sem, 1)
                return piece

            def split_terms(side):
                def piece(act, row):
                    roped.wait(act, row)
                    terms_T.wait(act, row, side + 1, back=1)
                    places = terms[side][:, :, 0:2 * HD if side == 0 else 3 * HD]
                    places = places.rearrange("p h (t d) -> p h t d", d=HD)
                    places = places if side == 0 else places[:, :, 0:3:2, :]
                    nc.scalar.activation(places, qk[:, side].rearrange("p h (a d) -> p h a d", a=1)
                                         .broadcast_to([P, HEADS, 2, HD]), ACT.Copy).then_inc(term_hi.sem, 1)
                return piece

            def copy_qT(act, row):
                terms_T.wait(act, row, 1)
                scored.wait(act, row, back=1)
                nc.scalar.activation(termT[0][:].rearrange("p j n -> p (j n)"), ring(2).bitcast(F16), ACT.Copy)\
                    .then_inc(qT_ready.sem, 1)

            def split_v(act, row):
                v_done.wait(act, row)
                av_ready.wait(act, row, back=1)
                nc.scalar.activation(v_cat[:, :, 0:HD], v_f[:], ACT.Copy).then_inc(v_hi.sem, 1)

            def exp_probs(g):
                def piece(act, row):
                    maxed.wait(act, row, g + 1)
                    probs_T.wait(act, row, g + 1, back=1)
                    for s in range(4):
                        last = nc.scalar.activation(sm[:, g, s, :], ring(2 + g % 2)[:, s * P:(s + 1) * P],
                                                    ACT.Exp, bias=mx[:, g, s:s + 1])
                    last.then_inc(exped.sem, 1)
                return piece

            def copy_probs(g):
                def piece(act, row):
                    probs_T.wait(act, row, g + 1)
                    av_ready.wait(act, row, back=1)
                    nc.scalar.activation(pT[0][:, g, :, :].rearrange("p s n -> p (s n)"), ring(2 + g % 2),
                                         ACT.Copy).then_inc(pT_hi.sem, 1)
                return piece

            def split_kv(half):
                def piece(act, row):
                    kv_ready.wait(act, row, half + 1)
                    conv_ready.wait(act, row, half + 1, back=1)
                    groups = slice(8 * half, 8 * half + 8)
                    nc.scalar.activation(kvh[0][:, :, groups, :], kv[:, :, groups, :], ACT.Copy)\
                        .then_inc(kv_hi.sem, 1)
                return piece

            def copy_vT(act, row):
                v_T.wait(act, row)
                kv_ready.wait(act, row, back=1)
                sk_mul.wait(act, row, 1, back=1)
                nc.scalar.activation(vT[:].rearrange("p c n -> p (c n)"), ring(0)[:, 0:E],
                                     ACT.Copy).then_inc(vT_ready.sem, 1)

            def moe_x_hi(act, row):
                xn3_T.wait(act, row)
                if not (isinstance(row.b, int) and row.b < 2):
                    up_ready.wait(act, row, back=2)
                nc.scalar.activation(xT[row.par][0][:].rearrange("p c n -> p (c n)"), ring(1)[:, 0:E],
                                     ACT.Copy).then_inc(xT_hi.sem, 1)

            def gate_tanh(act, row):
                routed.wait(act, row)
                cw_ready.wait(act, row, 1, back=1)
                nc.scalar.activation(gth[:], ring(0)[:, EXPERTS:NR], ACT.Tanh, scale=0.5 / WS)\
                    .then_inc(gth_ready.sem, 1)

            def router_exp(act, row):
                lmax_ready.wait(act, row)
                sel_done.wait(act, row, back=1)
                nc.scalar.activation(ex[:], lg[:, 0:EXPERTS], ACT.Exp, bias=lmax[:]).then_inc(ex_ready.sem, 1)

            def gate(act, row, c):
                gate_ready.wait(act, row, c + 1)
                if isinstance(row.b, int) and row.b == 0 and c == 0:
                    act.wait_ge(s_w_lo, NC * UNITS)
                if c == 0:
                    gate_done.wait(act, row, back=1)
                else:
                    gate_done.wait(act, row, c)
                nc.scalar.activation(th[:, 0:width(c)], pg[:, 0:width(c)], ACT.Tanh, scale=0.5 / WS).then_inc(tanh_done.sem, 1)

            def turn(act, row, c):
                inner_T.wait(act, row, c + 1)
                if c == 0:
                    down_done.wait(act, row, back=1)
                else:
                    down_done.wait(act, row, c)
                nc.scalar.activation(hT[0][:].rearrange("p t n -> p (t n)"), ph[:, 0:CHUNK],
                                     ACT.Copy).then_inc(inner_hi.sem, 1)

            act.wait_ge(s_half, 1)
            nc.scalar.activation(gth[:], minus_half[:], ACT.Tanh).then_inc(s_tables, 1)
            for kc in range(KC):
                act.wait_ge(s_wa[kc], 16)
                nc.scalar.activation(wa[0][:, kc, :], stage_a[:, kc * AW:(kc + 1) * AW], ACT.Copy,
                                     scale=WS).then_inc(s_wa_hi, 1)

            def split_toeplitz(act):
                act.wait_ge(s_toep, 16)
                nc.scalar.activation(toep_w[0][:].rearrange("p g c n -> p (g c n)"), scratch[:], ACT.Copy,
                                     scale=WS).then_inc(s_t_hi, 1)

            def prepare(act, u):
                if u == TOEP:
                    return split_toeplitz(act)
                c, n = divmod(u, UNITS)
                act.wait_ge(s_stage[u % RING], 16 * (u // RING + 1))
                nc.scalar.activation(unit_of(0, c, n), stage[:, u % RING], ACT.Copy, scale=WS)\
                    .then_inc(s_w_hi, 1)

            pieces = {0: [(MOE, gate_tanh)], 0.3: [(MOE, router_exp)], 1: [(MIX, lhs_split(1))], 1.3: [(ATT, lhs_split(0))],
                      2.3: [(MIX, copy_vT)], 3: [(ATT, split_terms(0)), (ATT, split_terms(1)), (MIX, split_kv(0))],
                      3.3: [(ATT, copy_qT), (ATT, split_v)],
                      3.6: [(ATT, exp_probs(0)), (ATT, exp_probs(1))], 4: [(MIX, split_kv(1))],
                      4.3: [(ATT, exp_probs(2)), (ATT, exp_probs(3))],
                      5.3: [(ATT, copy_probs(0)), (ATT, copy_probs(1))],
                      6.3: [(ATT, copy_probs(2)), (MIX, moe_x_hi), (ATT, copy_probs(3))]}
            steps(act, pieces, gate, turn, none, none, none, prepare=prepare, plans=(
                {2: [0, 1, 2, 3], 3.6: [TOEP], 4.3: [4, 5], 5.3: [6, 7], 6: [8], 6.3: [9]},
                {0: [10], 0.6: [11], 2: [12, 13], 3: [14], 3.6: [15, 16, 17], 4.3: [18, 19], 5.3: [20]}))

        @block.vector
        def _(dve):
            def norm(n, src_of, ready, used):
                def stats(dve, row):
                    ready(dve, row)
                    nc.vector.bn_stats(st6[n][:], src_of(row)).then_inc(ln_step[n].sem, 1)

                def aggregate(dve, row):
                    wait_apart(dve, (ln_step[n].sem, ln_step[n].value(row, 1)))
                    nc.vector.bn_aggr(mv[n][:], st6[n][:]).then_inc(ln_step[n].sem, 1)

                def variance(dve, row):
                    ln_step[n].wait(dve, row, 2)
                    nc.vector.tensor_scalar(var[n][:], mv[n][:, 1:2], EPS, None, ALU.add)\
                        .then_inc(ln_step[n].sem, 1)

                def result(dve, row):
                    rstd_ready[n].wait(dve, row)
                    used.wait(dve, row, back=1)
                    nc.vector.tensor_scalar(xn[n][:], src_of(row), mv[n][:, 0:1], rstd[n][:],
                                            ALU.subtract, ALU.mult).then_inc(normed[n].sem, 1)
                return stats, aggregate, variance, result

            norm1 = norm(0, lambda row: x_sb[row.par][:],
                         lambda dve, row: dve.wait_ge(s_x[row.par], row.half * 16 + 16), xn_T)
            norm2 = norm(1, lambda row: x1[:], lambda dve, row: x1_ready.wait(dve, row), v_T)
            norm3 = norm(2, lambda row: x2[row.par][:], lambda dve, row: x2_ready.wait(dve, row), xn3_T)

            def lhs_split(n):
                def piece(dve, row):
                    lhs_hi.wait(dve, row, n + 1)
                    nc.vector.tensor_tensor(tT[1][:].rearrange("p c n -> p (c n)"), ring(3)[:, 0:E],
                                            tT[0][:].rearrange("p c n -> p (c n)"), ALU.subtract)\
                        .then_inc(lhs_lo.sem, 1)
                return piece

            def v_bias(dve, row):
                v_ready.wait(dve, row)
                nc.vector.scalar_tensor_tensor(
                    out=v_f[:], in0=ring(3)[:, 0:E].rearrange("p (h d) -> p h d", d=HD), scalar=1.0 / WS,
                    in1=bv_sb[:].rearrange("p (h d) -> p h d", d=HD), op0=ALU.mult, op1=ALU.add)\
                    .then_inc(v_done.sem, 1)

            def split_v(dve, row):
                v_hi.wait(dve, row)
                nc.vector.tensor_tensor(v_cat[:, :, HD + 1:VW], v_f[:], v_cat[:, :, 0:HD], ALU.subtract)\
                    .then_inc(v_lo.sem, 1)

            def split_probs(g):
                def piece(dve, row):
                    pT_hi.wait(dve, row, g + 1)
                    nc.vector.tensor_tensor(pT[1][:, g, :, :].rearrange("p s n -> p (s n)"), ring(2 + g % 2),
                                            pT[0][:, g, :, :].rearrange("p s n -> p (s n)"), ALU.subtract)\
                        .then_inc(pT_lo.sem, 1)
                return piece

            def bias_qk(dve, row):
                qk_ready.wait(dve, row)
                sin_done.wait(dve, row, back=1)
                nc.vector.scalar_tensor_tensor(out=qkb[:].rearrange("p s h d -> p (s h d)"), in0=ring(2),
                                               scalar=1.0 / WS, in1=bqk_sb[:], op0=ALU.mult, op1=ALU.add)\
                    .then_inc(qk_biased.sem, 1)

            def rope_cos(dve, row):
                qk_biased.wait(dve, row)
                term_hi.wait(dve, row, back=1)
                nc.vector.tensor_tensor(qk[:], qkb[:], trig_sb[:, :, 0:1, :].broadcast_to([P, 2, HEADS, HD]),
                                        ALU.mult).then_inc(cos_done.sem, 1)

            def rope_sum(dve, row):
                cos_done.wait(dve, row)
                sin_done.wait(dve, row)
                nc.vector.tensor_tensor(qk[:], qk[:], rs[:], ALU.add).then_inc(roped.sem, 1)

            def split_terms(side):
                def piece(dve, row):
                    term_hi.wait(dve, row, side + 1)
                    at = 2 * HD if side == 0 else HD
                    nc.vector.tensor_tensor(terms[side][:, :, at:at + HD], qk[:, side], terms[side][:, :, 0:HD],
                                            ALU.subtract).then_inc(term_lo.sem, 1)
                return piece

            def copy_kT(dve, row):
                terms_T.wait(dve, row, 2)
                scored.wait(dve, row, back=1)
                nc.vector.tensor_copy(termT[1][:].rearrange("p j n -> p (j n)"), ring(3).bitcast(F16))\
                    .then_inc(kT_ready.sem, 1)

            def row_max(g):
                def piece(dve, row):
                    scored.wait(dve, row, g // 2 + 1)
                    nc.vector.tensor_reduce(mx[:, g, :], ring(2 + g % 2).rearrange("p (s n) -> p s n", n=P), X,
                                            ALU.max, negate=True).then_inc(maxed.sem, 1)
                return piece

            def normalise(dve, row):
                av_ready.wait(dve, row)
                o = pf[:, 2:4, 0:HEADS // 2 * VW].rearrange("p b (h d) -> p b h d", d=VW)
                out_heads = o_sb[:].rearrange("p (b h d) -> p b h d", b=2, d=HD)
                recips = rsum[:].rearrange("p (b h a) -> p b h a", b=2, a=1)
                o_T.wait(dve, row, back=1)
                nc.vector.tensor_copy(out_heads, o[:, :, :, HD + 1:VW]).then_inc(o_summed.sem, 1)
                nc.vector.reciprocal(recips, o[:, :, :, HD:HD + 1]).then_inc(recip_done.sem, 1)
                o_summed.wait(dve, row, 1)
                nc.vector.tensor_tensor(out_heads, out_heads, o[:, :, :, 0:HD], ALU.add).then_inc(o_summed.sem, 1)
                o_summed.wait(dve, row)
                recip_done.wait(dve, row)
                nc.vector.tensor_tensor(out_heads, out_heads, recips.broadcast_to([P, 2, HEADS // 2, HD]),
                                        ALU.mult).then_inc(o_ready.sem, 1)

            def residual1(dve, row):
                wo_ready.wait(dve, row)
                xb_ready.wait(dve, row)
                x2_ready.wait(dve, row, back=1)
                nc.vector.scalar_tensor_tensor(out=x1[:], in0=ring(2)[:, 0:E], scalar=1.0 / WS, in1=xb[:],
                                               op0=ALU.mult, op1=ALU.add).then_inc(x1_ready.sem, 1)

            def skip_sum(dve, row):
                sk_mul.wait(dve, row)
                sk_out.wait(dve, row, back=1)
                nc.vector.tensor_reduce(sks[:].rearrange("p c g -> p (c g)"),
                                        sk2[:].rearrange("p c (g i) -> p (c g) i", i=SIDE),
                                        X, ALU.add).then_inc(sk_sum.sem, 1)

            def gate_conv(half, c):
                def piece(dve, row):
                    k = 2 * half + c
                    conv_ready.wait(dve, row, half + 1)
                    if k > 0:
                        gsum.wait(dve, row, k)
                    else:
                        gsum.wait(dve, row, back=1)
                        o2_ready.wait(dve, row, back=1)
                    G2 = GROUPS // 2
                    y = pf[:, 0:2, :].rearrange("p b (h c n) -> p (b h) c n", h=4, c=2)[:, :, c, :]
                    y = y.rearrange("p h (j i) -> p h j i", i=SIDE)
                    cT = c_sb[row.par][:, c, half * 64:half * 64 + 64].rearrange("p (h a i) -> p h a i", a=1, i=SIDE)
                    zz = z[:, k % 2 * 512:k % 2 * 512 + 512].rearrange("p (h j i) -> p h j i", j=SIDE, i=SIDE)
                    nc.vector.tensor_tensor(zz, y, cT.broadcast_to([P, G2, SIDE, SIDE]), ALU.mult)\
                        .then_inc(gated.sem, 1)
                    gated.wait(dve, row, k + 1)
                    nc.vector.tensor_reduce(o2[:, c, half * 64:half * 64 + 64],
                                            z[:, k % 2 * 512:k % 2 * 512 + 512].rearrange("p (n i) -> p n i", i=SIDE),
                                            X, ALU.add).then_inc(gsum.sem, 1)
                return piece

            def residual2(dve, row):
                o2_T.wait(dve, row)
                if not (isinstance(row.b, int) and row.b < 2):
                    dve.wait_ge(s_y[row.par], row.half * 16)
                nc.vector.scalar_tensor_tensor(out=x2[row.par][:], in0=ring(0)[:, 0:E], scalar=1.0 / WS, in1=x1[:],
                                               op0=ALU.mult, op1=ALU.add).then_inc(x2_ready.sem, 1)

            def moe_x_lo(dve, row):
                xT_hi.wait(dve, row)
                nc.vector.tensor_tensor(xT[row.par][1][:].rearrange("p c n -> p (c n)"), ring(1)[:, 0:E],
                                        xT[row.par][0][:].rearrange("p c n -> p (c n)"), ALU.subtract)\
                    .then_inc(xT_lo.sem, 1)

            def logits(dve, row):
                gth_ready.wait(dve, row)
                ex_ready.wait(dve, row, back=1)
                nc.vector.tensor_scalar(lg[:, 0:EXPERTS], ring(0)[:, 0:EXPERTS], 1.0 / WS, None, ALU.mult)\
                    .then_inc(lg_ready.sem, 1)
                inner_done.wait(dve, row, back=2)
                nc.vector.tensor_scalar(cw[row.par][:, EXPERTS:NR], gth[:], 1.0, 0.5 * SILU, ALU.add, ALU.mult)\
                    .then_inc(cw_ready.sem, 1)

            def top(dve, row):
                wait_apart(dve, (lg_ready.sem, lg_ready.value(row)))
                nc.vector.max(top8[:], lg[:, 0:EXPERTS]).then_inc(top_ready.sem, 1)
                top_ready.wait(dve, row)
                nc.vector.tensor_scalar(lmax[:], top8[:, 0:1], -1.0, None, ALU.mult).then_inc(lmax_ready.sem, 1)

            def pick_values(dve, row):
                nc.vector.tensor_copy(picks[:, 0:TOP], top8[:, 0:TOP]).then_inc(pick_done.sem, 1)

            def mark_picked(dve, row):
                wait_apart(dve, (pick_done.sem, pick_done.value(row, 1)))
                nc.vector.match_replace(out=picked[:], in_to_replace=picks[:], in_values=lg[:], imm_value=-NEG)\
                    .then_inc(pick_done.sem, 1)

            def select(dve, row):
                pick_done.wait(dve, row, 2)
                ex_ready.wait(dve, row)
                nc.vector.scalar_tensor_tensor(out=esel[:], in0=picked[:, 0:EXPERTS], scalar=-NEG, in1=ex[:],
                                               op0=ALU.is_equal, op1=ALU.mult).then_inc(sel_done.sem, 1)

            def select_sum(dve, row):
                sel_done.wait(dve, row, 1)
                nc.vector.reduce_sum(esum[:], esel[:], X).then_inc(sel_done.sem, 1)

            def select_recip(dve, row):
                sel_done.wait(dve, row, 2)
                nc.vector.reciprocal(erec[:], esum[:]).then_inc(sel_done.sem, 1)

            def expert_weights(dve, row):
                sel_done.wait(dve, row, 3)
                nc.vector.tensor_scalar(cw[row.par][:, 0:EXPERTS], esel[:], erec[:], SILU, ALU.mult, ALU.mult)\
                    .then_inc(cw_ready.sem, 1)

            def gate(dve, row, c):
                tanh_done.wait(dve, row, c + 1)
                if c == 0:
                    inner_done.wait(dve, row, back=1)
                else:
                    inner_done.wait(dve, row, c)
                n = width(c)
                nc.vector.scalar_tensor_tensor(out=ga[:, 0:n], in0=th[:, 0:n], scalar=1.0, in1=pg[:, 0:n],
                                               op0=ALU.add, op1=ALU.mult).then_inc(gate_done.sem, 1)

            def turn(dve, row, c):
                inner_hi.wait(dve, row, c + 1)
                nc.vector.tensor_tensor(hT[1][:].rearrange("p t n -> p (t n)"), ph[:, 0:CHUNK],
                                        hT[0][:].rearrange("p t n -> p (t n)"), ALU.subtract)\
                    .then_inc(inner_lo.sem, 1)

            def up(dve, row, c):
                gate_done.wait(dve, row, c + 1)
                up_ready.wait(dve, row, c + 1)
                if c == 0:
                    inner_T.wait(dve, row, back=1)
                    cw_ready.wait(dve, row, 1)
                else:
                    inner_T.wait(dve, row, c)
                    if c == SHARED // CHUNK:
                        cw_ready.wait(dve, row)
                for lo, hi, e in segments(c):
                    last = nc.vector.scalar_tensor_tensor(
                        out=hh[:, lo:hi], in0=pu[:, lo:hi], scalar=cw[row.par][:, e:e + 1],
                        in1=ga[:, lo:hi], op0=ALU.mult, op1=ALU.mult)
                last.then_inc(inner_done.sem, 1)

            def finish(dve, row):
                down_done.wait(dve, row)
                nc.vector.scalar_tensor_tensor(out=x2[row.par][:], in0=pacc[:, 0:E], scalar=1.0 / WS,
                                               in1=x2[row.par][:], op0=ALU.mult, op1=ALU.add)\
                    .then_inc(y_ready.sem, 1)

            nc.vector.memset(v_cat[:, :, HD:HD + 1], 1.0).then_inc(s_once, 1)
            for side in range(2):
                nc.vector.memset(terms[side][:, :, 3 * HD:ROWS], 0.0).then_inc(s_once, 1)
            nc.vector.memset(lg[:, EXPERTS:], NEG).then_inc(s_once, 1)
            nc.vector.memset(picks[:, TOP:], NEG).then_inc(s_once, 1)
            dve.wait_ge(s_once, 5)
            dve.wait_ge(s_const, NCONST)
            nc.vector.tensor_copy(id_b[:], id_sb[:]).then_inc(s_once, 1)
            nc.vector.tensor_copy(id_h[:], id_sb[:]).then_inc(s_once, 1)
            nc.vector.tensor_copy(causal_b[:], causal_sb[:]).then_inc(s_once, 1)
            nc.vector.tensor_scalar(skip64[:], skip_sb[:], WS, None, ALU.mult).then_inc(s_once, 1)
            def split_attention(dve):
                for kc in range(KC):
                    dve.wait_ge(s_wa_hi, kc + 1)
                    nc.vector.scalar_tensor_tensor(out=wa[1][:, kc, :], in0=stage_a[:, kc * AW:(kc + 1) * AW],
                                                   scalar=WS, in1=wa[0][:, kc, :], op0=ALU.mult,
                                                   op1=ALU.subtract).then_inc(s_wa_lo, 1)

            def split_toeplitz(dve):
                dve.wait_ge(s_t_hi, 1)
                nc.vector.scalar_tensor_tensor(out=toep_w[1][:].rearrange("p g c n -> p (g c n)"), in0=scratch[:],
                                               scalar=WS, in1=toep_w[0][:].rearrange("p g c n -> p (g c n)"),
                                               op0=ALU.mult, op1=ALU.subtract).then_inc(s_t_lo, 1)

            def prepare(dve, u):
                if u == ATTN:
                    return split_attention(dve)
                if u == TOEP:
                    return split_toeplitz(dve)
                c, n = divmod(u, UNITS)
                dve.wait_ge(s_w_hi, u + 1)
                nc.vector.scalar_tensor_tensor(out=unit_of(1, c, n), in0=stage[:, u % RING], scalar=WS,
                                               in1=unit_of(0, c, n), op0=ALU.mult, op1=ALU.subtract)\
                    .then_inc(s_w_lo, 1)

            pieces = {0: [(MOE, logits), (MOE, top)],
                      0.3: [(MOE, pick_values), (MIX, normalise), (MOE, mark_picked), (ATT, norm1[0]), (MOE, select),
                            (ATT, norm1[1]), (MOE, select_sum), (ATT, norm1[2]), (MOE, select_recip),
                            (MOE, expert_weights)], 1: [(MIX, lhs_split(1)), (ATT, norm1[3])],
                      1.3: [(ATT, lhs_split(0)), (MIX, residual1), (MIX, norm2[0]), (MIX, norm2[1]), (MIX, norm2[2])],
                      2: [(MIX, norm2[3])],
                      2.3: [(ATT, bias_qk), (ATT, rope_cos), (ATT, v_bias), (ATT, rope_sum)],
                      3: [(ATT, split_terms(0)), (ATT, split_terms(1)), (ATT, copy_kT)], 3.3: [(ATT, split_v)],
                      3.6: [(ATT, row_max(0)), (ATT, row_max(1))],
                      3.8: [(MIX, gate_conv(0, 0)), (MIX, skip_sum)], 4: [(MIX, gate_conv(0, 1))],
                      4.3: [(ATT, row_max(2)), (ATT, row_max(3))],
                      4.6: [(MIX, gate_conv(1, 0))], 5: [(MIX, gate_conv(1, 1))],
                      5.3: [(ATT, split_probs(0))],
                      5.6: [(MIX, residual2), (MIX, norm3[0]), (MIX, norm3[1]), (MIX, norm3[2]), (ATT, split_probs(1))],
                      6: [(MIX, norm3[3])],
                      6.3: [(ATT, split_probs(2)), (MIX, moe_x_lo), (ATT, split_probs(3))]}
            steps(dve, pieces, gate, turn, up, none, finish, prepare=prepare, plans=(
                {1: [ATTN], 2: [0, 1], 3: [2], 3.3: [3], 4.3: [TOEP], 5.3: [4, 5], 6: [6, 7], 6.3: [8]},
                {0.3: [9], 0.6: [10], 1.3: [11], 2.3: [12, 13], 3: [14], 3.3: [15], 3.8: [16, 17], 4.3: [18], 4.6: [19], 5.3: [20]}))

        @block.gpsimd
        def _(pool):
            def add_bias(pool, row):
                pool.wait_ge(s_x[row.par], row.half * 16 + 16)
                x1_ready.wait(pool, row, back=1)
                nc.gpsimd.tensor_tensor(xb[:], x_sb[row.par][:], bo_sb[:], ALU.add).then_inc(xb_ready.sem, 1)

            def rope_sin(pool, row):
                qk_biased.wait(pool, row)
                roped.wait(pool, row, back=1)
                pairs = lambda t: t.rearrange("p s h (n two) -> p s h n two", two=2)
                for odd in range(2):
                    last = nc.gpsimd.tensor_tensor(
                        pairs(rs[:])[:, :, :, :, odd], pairs(qkb[:])[:, :, :, :, 1 - odd],
                        pairs(trig_sb[:, :, 1:2, :])[:, :, :, :, odd].broadcast_to([P, 2, HEADS, HD // 2]), ALU.mult)
                last.then_inc(sin_done.sem, 1)

            def products_kv(half):
                def piece(pool, row):
                    vT_ready.wait(pool, row)
                    pool.wait_ge(s_c[row.par], row.half * 16 + 16)
                    if isinstance(row.b, int) and row.b == 0:
                        pool.wait_ge(s_t_hi, 1)
                        pool.wait_ge(s_t_lo, 1)
                    G2 = GROUPS // 2
                    cols = slice(half * 64, half * 64 + 64)
                    for c in range(KC):
                        vs = vT[:, c, cols].rearrange("p (h a i) -> p h a i", a=1, i=SIDE)
                        cs = c_sb[row.par][:, c, cols].rearrange("p (h j a) -> p h j a", a=1, j=SIDE)
                        last = nc.gpsimd.tensor_tensor(
                            kv[:, c, half * G2:(half + 1) * G2, :].rearrange("p h (j i) -> p h j i", i=SIDE),
                            cs.broadcast_to([P, G2, SIDE, SIDE]), vs.broadcast_to([P, G2, SIDE, SIDE]), ALU.mult)
                    last.then_inc(kv_ready.sem, 1)
                return piece

            def split_kv(half):
                def piece(pool, row):
                    kv_hi.wait(pool, row, half + 1)
                    groups = slice(8 * half, 8 * half + 8)
                    nc.gpsimd.tensor_tensor(kvh[1][:, :, groups, :], kv[:, :, groups, :], kvh[0][:, :, groups, :],
                                            ALU.subtract).then_inc(kv_lo.sem, 1)
                return piece

            def skip_products(pool, row):
                sk_sum.wait(pool, row, back=1)
                nc.gpsimd.tensor_tensor(sk1[:], vT[:], c_sb[row.par][:], ALU.mult).then_inc(sk_mul.sem, 1)
                sk_mul.wait(pool, row, 1)
                nc.gpsimd.tensor_tensor(sk2[:], sk1[:],
                                        skip64[:].rearrange("p (a n) -> p a n", a=1).broadcast_to([P, KC, P]),
                                        ALU.mult).then_inc(sk_mul.sem, 1)

            def skip_out(pool, row):
                sk_sum.wait(pool, row)
                o2_ready.wait(pool, row, back=1)
                nc.gpsimd.tensor_tensor(skc[:].rearrange("p c (g j) -> p (c g) j", j=SIDE),
                                        c_sb[row.par][:].rearrange("p c (g j) -> p (c g) j", j=SIDE),
                                        sks[:].rearrange("p c (g a) -> p (c g) a", a=1)
                                        .broadcast_to([P, KC * GROUPS, SIDE]), ALU.mult).then_inc(sk_out.sem, 1)

            def conv_out(pool, row):
                gsum.wait(pool, row)
                sk_out.wait(pool, row)
                o2_T.wait(pool, row, back=1)
                nc.gpsimd.tensor_tensor(o2f[:], o2[:], skc[:], ALU.add).then_inc(o2_ready.sem, 1)

            def root(n):
                def piece(pool, row):
                    ln_step[n].wait(pool, row)
                    nc.gpsimd.tensor_tensor(rstd[n][:], var[n][:], minus_half[:], ALU.pow)\
                        .then_inc(rstd_ready[n].sem, 1)
                return piece

            nc.gpsimd.memset(minus_half[:], -0.5).then_inc(s_half, 1)
            pool.wait_ge(s_half, 1)
            pool.wait_ge(s_once, 9)
            pool.wait_ge(s_const, NCONST)
            pieces = {0: [(ATT, root(0))], 1.3: [(MIX, root(1))],
                      2.3: [(ATT, rope_sin), (MIX, products_kv(0)), (MIX, split_kv(0)), (MIX, products_kv(1)),
                            (MIX, skip_products), (MIX, split_kv(1))],
                      4.6: [(MIX, skip_out)], 5: [(MIX, conv_out)], 5.6: [(MIX, root(2)), (ATT, add_bias)]}
            steps(pool, pieces, none, none, none, none, none)


def rope_tables():
    pos = np.arange(P, dtype=np.float32)[:, None]
    exps = -np.arange(0, HD, 2, dtype=np.float32) / np.float32(HD)
    thetas = np.repeat(np.power(np.float32(10000.0), exps), 2)
    angles = (pos * thetas[None, :]).astype(np.float32)
    sign = np.where(np.arange(HD) % 2 == 0, -1.0, 1.0)
    both = np.stack([np.cos(angles), np.sin(angles) * sign], axis=1).astype(np.float32)
    return np.stack([both * np.float32(HD ** -0.5), both], axis=1)


def constants():
    at = np.arange(P)
    return {
        "trig": rope_tables(),
        "causal": np.where(at[None, :] > at[:, None], NEG, 0.0).astype(np.float32),
        "ident": np.eye(P, dtype=np.float32),
    }


def by_rows(w):
    return w.reshape(KC, P, -1).transpose(1, 0, 2)


def attention_weights(Wq, Wk, Wv, Wo, gate_w, gate_vec):
    pad = np.zeros((E, AW - R0 - NR), np.float32)
    w = np.concatenate([Wq, Wk, Wv, Wo, gate_w.T, gate_vec.T, pad], axis=1)
    return by_rows(w).reshape(P, KC * AW)


def expert_weights(egu, ed, sgu, sd):
    gates = np.concatenate([sgu[:SHARED], egu[:, :INTER].reshape(-1, E)])
    ups = np.concatenate([sgu[SHARED:], egu[:, INTER:].reshape(-1, E)])
    downs = np.concatenate([sd.T, ed.transpose(0, 2, 1).reshape(-1, E)])
    gates, ups, downs = (np.concatenate([w, np.zeros((NCHUNK * CHUNK - INNER, E), np.float32)])
                         for w in (gates, ups, downs))
    gu = np.stack([gates.reshape(NCHUNK, CHUNK, KC, P), ups.reshape(NCHUNK, CHUNK, KC, P)])
    gu = gu.transpose(1, 3, 4, 0, 2).reshape(NCHUNK, KC, P, UNIT)
    dn = downs.reshape(NCHUNK, DT, P, E).transpose(0, 2, 1, 3).reshape(NCHUNK, 1, P, UNIT)
    return np.concatenate([gu, dn], axis=1).reshape(NCHUNK * UNITS, P, UNIT)


def toeplitz(k):
    padded = np.concatenate([np.zeros((GROUPS, P - 1), np.float32), k], axis=1)
    at = P - 1 + np.arange(2 * P)[None, :] - np.arange(P)[:, None]
    return padded[:, at].transpose(1, 0, 2).reshape(P, GROUPS, 2, P)


def kernel(**inputs):
    import concourse.bacc as bacc
    from concourse.bass_utils import run_bass_kernel_spmd

    a = {n: np.asarray(v) for n, v in inputs.items()}
    arrays = {
        "x": a["x"],
        "ctx_in": a["ctx_2048"].reshape(-1, P, KC, P).transpose(0, 3, 2, 1),
        "w_attn": attention_weights(a["L0_attn_Wq"], a["L0_attn_Wk"], a["L0_attn_Wv"], a["L0_attn_Wo"],
                                    a["L0_ffn_gate_w"], a["L0_ffn_shared_gate_vec"]),
        "w_moe": expert_weights(a["L0_ffn_expert_gate_up"], a["L0_ffn_expert_down"],
                                a["L0_ffn_shared_gate_up"], a["L0_ffn_shared_down"]),
        "toep": toeplitz(a["L0_xattn_k"]),
        "bias_qk": np.concatenate([a["L0_attn_bq"], a["L0_attn_bk"]]),
        "bias_v": a["L0_attn_bv"], "bias_o": a["L0_attn_bo"], "skip": a["fside_S2_0"],
        **constants(),
    }
    nc = bacc.Bacc("TRN2", target_bir_lowering=False, num_devices=1)
    args = {}
    arrays = {f"in_{n}": np.ascontiguousarray(v) for n, v in arrays.items()}
    for n, v in arrays.items():
        args[n[3:]] = nc.dram_tensor(n, v.shape, mybir.dt.from_np(v.dtype), kind="ExternalInput").ap()
    out = nc.dram_tensor("out_y", a["x"].shape, F32, kind="ExternalOutput").ap()
    build(nc, out=out, **args)
    r = run_bass_kernel_spmd(nc, [arrays], core_ids=[0])
    return r.results[0]["out_y"]
```
